# Optimizing a Trainium2 kernel written in Bass

```python
import numpy as np
import jax
import jax.numpy as jnp

def _softmax(x, axis=-1):
    return jax.nn.softmax(x, axis=axis)

def _gelu(x):
    return jax.nn.gelu(x, approximate=True)

def _silu(x):
    return jax.nn.silu(x)

def _sigmoid(x):
    return jax.nn.sigmoid(x)

def _layernorm(x, axis=-1, eps=1e-05):
    m = jnp.mean(x, axis=axis, keepdims=True)
    v = jnp.var(x, axis=axis, keepdims=True)
    return (x - m) / jnp.sqrt(v + eps)

def _scatter_add(tgt, idx, src, axis=0):
    return tgt.at[idx].add(src)

def _segment_sum(src, seg, n):
    return jax.ops.segment_sum(src, seg, n)
kernel_name = 'mk_cond_resid_d2_seqx_r4_254f24'

def setup_inputs(seed: int=0):
    np.random.seed(seed)
    _w = jnp.asarray

    def _rec_inputs():
        import jax
        import jax.numpy as jnp
        _rk = jax.random.key(seed)
        x = 4.136e-05 + 0.9999 * jax.random.normal(jax.random.fold_in(_rk, 1), (32, 256, 256), jnp.float32)
        _lenS = 256 - jax.random.randint(jax.random.fold_in(_rk, 7), (32,), 0, max(1, 256 // 4) + 1, jnp.int32)
        _lenS2 = 256 - jax.random.randint(jax.random.fold_in(_rk, 8), (32,), 0, max(1, 256 // 4) + 1, jnp.int32)
        cond_1024 = -0.00499425 + 1.0058 * jax.random.normal(jax.random.fold_in(_rk, 11), (32, 256), jnp.float32)
        return (x, cond_1024)
    x, cond_1024 = _rec_inputs()

    def _L0_cond_setup():
        import jax, jax.numpy as jnp
        import numpy as np
        B, N, D, C = (32, 64, 256, 256)
        key = jax.random.key(seed)
        k1, k2, k3, k4 = jax.random.split(key, 4)
        scale = 1.0 / np.sqrt(D)
        return {'encoded_utterance': jax.random.normal(k1, (B, D), dtype=jnp.float32), 'element_embeddings': jax.random.normal(k2, (B, N, D), dtype=jnp.float32), 'weight_matrix': jax.random.normal(k3, (2 * D, C), dtype=jnp.float32) * scale, 'W_proj': jax.random.normal(k4, (D, D), dtype=jnp.float32) * scale, 'b_proj': jnp.zeros((D,), dtype=jnp.float32)}
    _L0_cond_all = _L0_cond_setup()
    _L0_cond_in = {k: v for k, v in _L0_cond_all.items() if k in ('weight_matrix', 'W_proj', 'b_proj')}
    del _L0_cond_all

    def _L1_cond_setup():
        import jax, jax.numpy as jnp
        import numpy as np
        D = 256
        key = jax.random.key(seed)
        ks = jax.random.split(key, 12)
        sc_in = 1.0 / np.sqrt(D)
        sc_in2 = 1.0 / np.sqrt(2 * D)
        inp = {'X1': jax.random.normal(ks[0], (8, D), dtype=jnp.float32), 'X2': jax.random.normal(ks[1], (8, 512, D), dtype=jnp.float32), 'Wq1': jax.random.normal(ks[2], (D, D), dtype=jnp.float32) * sc_in, 'bq1': jax.random.normal(ks[3], (D,), dtype=jnp.float32) * 0.01, 'Wq2': jax.random.normal(ks[4], (D, D), dtype=jnp.float32) * sc_in, 'bq2': jax.random.normal(ks[5], (D,), dtype=jnp.float32) * 0.01, 'Wk1': jax.random.normal(ks[6], (D, D), dtype=jnp.float32) * sc_in, 'bk1': jax.random.normal(ks[7], (D,), dtype=jnp.float32) * 0.01, 'Wk2': jax.random.normal(ks[8], (D, D), dtype=jnp.float32) * sc_in, 'bk2': jax.random.normal(ks[9], (D,), dtype=jnp.float32) * 0.01, 'Wv': jax.random.normal(ks[10], (2 * D, D), dtype=jnp.float32) * sc_in2, 'bv': jax.random.normal(ks[11], (D,), dtype=jnp.float32) * 0.01, 'alpha': jnp.float32(0.5)}
        return inp
    _L1_cond_all = _L1_cond_setup()
    _L1_cond_in = {k: v for k, v in _L1_cond_all.items() if k in ('Wq1', 'bq1', 'Wq2', 'bq2', 'Wk1', 'bk1', 'Wk2', 'bk2', 'Wv', 'bv', 'alpha')}
    del _L1_cond_all
    return {'x': x, 'cond_1024': cond_1024, 'L0_cond_weight_matrix': _L0_cond_in['weight_matrix'], 'L0_cond_W_proj': _L0_cond_in['W_proj'], 'L0_cond_b_proj': _L0_cond_in['b_proj'], 'L1_cond_Wq1': _L1_cond_in['Wq1'], 'L1_cond_bq1': _L1_cond_in['bq1'], 'L1_cond_Wq2': _L1_cond_in['Wq2'], 'L1_cond_bq2': _L1_cond_in['bq2'], 'L1_cond_Wk1': _L1_cond_in['Wk1'], 'L1_cond_bk1': _L1_cond_in['bk1'], 'L1_cond_Wk2': _L1_cond_in['Wk2'], 'L1_cond_bk2': _L1_cond_in['bk2'], 'L1_cond_Wv': _L1_cond_in['Wv'], 'L1_cond_bv': _L1_cond_in['bv'], 'L1_cond_alpha': _L1_cond_in['alpha']}

def reference(x, cond_1024, L0_cond_weight_matrix, L0_cond_W_proj, L0_cond_b_proj, L1_cond_Wq1, L1_cond_bq1, L1_cond_Wq2, L1_cond_bq2, L1_cond_Wk1, L1_cond_bk1, L1_cond_Wk2, L1_cond_bk2, L1_cond_Wv, L1_cond_bv, L1_cond_alpha):
    import jax
    import jax.numpy as jnp

    def _L0_cond_ref(encoded_utterance, element_embeddings, weight_matrix, W_proj, b_proj):
        import jax, jax.numpy as jnp
        import numpy as np
        B, N, D, C = (32, 64, 256, 256)
        u = jax.nn.gelu(encoded_utterance @ W_proj + b_proj, approximate=False)
        W_u, W_e = (weight_matrix[:D], weight_matrix[D:])
        logits = (u @ W_u)[:, None, :] + jnp.einsum('bnd,dc->bnc', element_embeddings, W_e)
        return logits

    def _L1_cond_ref(X1, X2, Wq1, bq1, Wq2, bq2, Wk1, bk1, Wk2, bk2, Wv, bv, alpha):
        import jax, jax.numpy as jnp
        import numpy as np
        D = 256
        B, S, Dm = X2.shape
        X1e = jnp.broadcast_to(X1[:, None, :], (B, S, Dm))
        X = jnp.concatenate([X1e, X2], axis=-1)
        Q1 = X1e @ Wq1 + bq1
        K1 = X1e @ Wk1 + bk1
        Q2 = X2 @ Wq2 + bq2
        K2 = X2 @ Wk2 + bk2
        V = X @ Wv + bv
        s = 1.0 / jnp.sqrt(jnp.float32(Dm))
        A1 = jnp.einsum('bqd,bkd->bqk', Q1, K1) * s
        A2 = jnp.einsum('bqd,bkd->bqk', Q2, K2) * s
        A = jax.nn.softmax(A2, axis=-1) - alpha * jax.nn.softmax(A1, axis=-1)
        return jnp.einsum('bqk,bkd->bqd', A, V)
    x = x + _L0_cond_ref(cond_1024, x, L0_cond_weight_matrix, L0_cond_W_proj, L0_cond_b_proj)
    x = x + _L1_cond_ref(cond_1024, x, L1_cond_Wq1, L1_cond_bq1, L1_cond_Wq2, L1_cond_bq2, L1_cond_Wk1, L1_cond_bk1, L1_cond_Wk2, L1_cond_bk2, L1_cond_Wv, L1_cond_bv, L1_cond_alpha)
    return x

_drawn_inputs = setup_inputs


def setup_inputs(seed=0):
    import zlib

    import numpy as np

    out = dict(_drawn_inputs(seed))
    spreads = {'L0_cond_b_proj': (0.0, 0.1)}
    factors = {'L1_cond_bq2': 24.952, 'L1_cond_bk2': 64.0, 'L1_cond_bv': 8.0}
    for name, (base, spread) in spreads.items():
        noise = np.random.default_rng([zlib.crc32(name.encode()), seed]).standard_normal(out[name].shape)
        drawn = base * np.exp(spread * noise) if base else spread * noise
        out[name] = jnp.asarray(drawn.astype(out[name].dtype))
    for name, factor in factors.items():
        out[name] = (out[name] * factor).astype(out[name].dtype)
    return out
```

```python
from contextlib import ExitStack

import concourse.bass as bass
from concourse import mybir

ALU = mybir.AluOpType
ACT = mybir.ActivationFunctionType
AX = mybir.AxisListType
F32 = mybir.dt.float32
F32R = mybir.dt.float32r
P = 128




def build(nc, x, cond, Wul, Wp, bp, Wq1, bq1, Wq2, bq2, Wk1, bk1, Wk2, bk2, Wv, bv, alpha, out):
    B, S, D = x.shape
    DT = D // P
    ST = S // P
    SCALE = float(D) ** -0.5
    assert DT == 2 and ST == 2 and B % 2 == 0 and B >= 6
    BIAS = {"bp": bp, "bq1": bq1, "bk1": bk1, "bq2": bq2, "bk2": bk2, "bv": bv}
    BROW = {n: i for i, n in enumerate(BIAS)}

    x_rows = x.rearrange("b (p t) d -> b p (t d)", t=ST)
    out_rows = out.rearrange("b (p t) d -> b p (t d)", t=ST)

    with ExitStack() as ctx:
        def sb(name, shape, dt=F32):
            return ctx.enter_context(nc.sbuf_tensor(name, shape, dt))

        def ps(name, shape):
            return ctx.enter_context(nc.psum_tensor(name, shape, F32))

        def sem(name):
            return ctx.enter_context(nc.semaphore(name))

        we_in = sb("we_in", [P, DT, D])
        wu_in = sb("wu_in", [P, DT, D])
        wp_in = sb("wp_in", [P, DT, D])
        wq1_in = sb("wq1_in", [P, DT, D])
        wk1_in = sb("wk1_in", [P, DT, D])
        wq2_in = sb("wq2_in", [P, DT, D])
        wk2_in = sb("wk2_in", [P, DT, D])
        wv_in = sb("wv_in", [P, 2, DT, D])
        cond_in = sb("cond_in", [B, D])
        bias_in = sb("bias_in", [1, len(BIAS), D])
        alpha_in = sb("alpha_in", [B, 1])
        ident = sb("ident", [P, P])
        eye = sb("eye", [P, DT, D])
        ones = sb("ones", [B, P])
        wT = sb("wT", [P, DT, D])
        w_nat = sb("w_nat", [P, DT, D])
        g1T = sb("g1T", [P, DT, D])
        g2T = sb("g2T", [P, DT, D])
        m_h = sb("m_h", [P, DT, D], F32R)
        m_l = sb("m_l", [P, DT, D], F32R)
        zw_h = sb("zw_h", [P, DT, 2 * D], F32R)
        zw_l = sb("zw_l", [P, DT, 2 * D], F32R)
        condT = sb("condT", [P, DT, B])
        uT = sb("uT", [P, DT, B])
        rT = sb("rT", [P, DT, B])
        aT = sb("aT", [P, DT, B])
        gT = sb("gT", [P, B, DT])
        r_row = sb("r_row", [B, D])
        q1 = sb("q1", [B, D])
        qk1 = sb("qk1", [B, D])
        a1 = sb("a1", [B, 8])
        ap_diag = sb("ap_diag", [B, B])
        ap_col = sb("ap_col", [P, B])
        row = sb("row", [B, D])
        row_flat = sb("row_flat", [1, B, D])
        row_all = sb("row_all", [P, B, D])
        x_nat = sb("x_nat", [P, 2, ST, D])
        x_h = sb("x_h", [P, 2, DT, S], F32R)
        x_l = sb("x_l", [P, 2, DT, S], F32R)
        t_h = sb("t_h", [P, DT, S], F32R)
        t_l = sb("t_l", [P, DT, S], F32R)
        v_h = sb("v_h", [P, ST, D], F32R)
        v_l = sb("v_l", [P, ST, D], F32R)
        neg_max = sb("neg_max", [P, ST])
        e_nat = sb("e_nat", [P, ST, S])
        den = sb("den", [P, ST])
        r_den = sb("r_den", [P, ST])
        a_nat = sb("a_nat", [P, ST, S])
        a_h = sb("a_h", [P, ST, S], F32R)
        a_l = sb("a_l", [P, ST, S], F32R)
        o_sb = sb("o_sb", [P, 2, ST, D])

        xt_ps = ps("xt_ps", [P, DT, S])
        t_ps = ps("t_ps", [P, DT, S])
        s_ps = ps("s_ps", [P, ST, S])
        at_ps = ps("at_ps", [P, ST, S])
        vo_ps = ps("vo_ps", [P, 2, ST, 2 * D])

        ld = {n: sem("ld_" + n) for n in ("we", "wu", "wp", "wq1", "wk1", "wq2", "wk2", "wv", "cond", "bias", "alpha")}
        x_loaded = [sem("x_loaded0"), sem("x_loaded1")]
        eye_zero = sem("eye_zero")
        eye_made = sem("eye_made")
        ones_made = sem("ones_made")
        prep_pe = {n: sem("pe_" + n) for n in ("condT", "wT", "u", "rT", "g1", "g2", "a", "m", "z", "g", "c", "k1", "ap")}
        prep_sb = {n: sem("sb_" + n) for n in ("condT", "wT", "u", "rT", "g1", "g2", "a", "mh", "ml", "zh", "zl",
                                               "g", "rrow", "wnat", "wh", "wl", "q1", "apcol")}
        a1_dve = sem("a1_dve")
        a1_exp = sem("a1_exp")
        row_made = sem("row_made")
        row_moved = sem("row_moved")
        row_spread = sem("row_spread")
        xt_done, t_done, s_done, v_done, at_done, av_done = (sem(n) for n in ("xt_done", "t_done", "s_done", "v_done", "at_done", "av_done"))
        xh_done, th_done, e_done, vh_done, ah_done = (sem(n) for n in ("xh_done", "th_done", "e_done", "vh_done", "ah_done"))
        xl_done, tl_done, max_done, rden_done, a_done, vl_done, al_done, o_done = (
            sem(n) for n in ("xl_done", "tl_done", "max_done", "rden_done", "a_done", "vl_done", "al_done", "o_done"))
        o_stored = [sem("o_stored0"), sem("o_stored1")]

        wT_ps = vo_ps[:, 0, 0, :].rearrange("p (t n) -> p t n", t=DT)
        g1_ps = vo_ps[:, 0, 1, :].rearrange("p (t n) -> p t n", t=DT)
        g2_ps = vo_ps[:, 1, 0, :].rearrange("p (t n) -> p t n", t=DT)
        z_ps = vo_ps[:, 1, 1, :].rearrange("p (t n) -> p t n", t=DT)
        m_ps = t_ps
        small = s_ps[:].rearrange("p t n -> p (t n)")

        def small_at(i):
            return small[:, i * DT * B:(i + 1) * DT * B].rearrange("p (t b) -> p t b", t=DT)

        condT_ps, u_ps, rT_ps, a_ps, g_ps = (small_at(i) for i in range(5))
        ap_ps = small[:, 5 * DT * B:5 * DT * B + B]
        q1_ps = at_ps[0:B, 0, :]
        k1_ps = at_ps[0:B, 1, :]
        rrow_ps = vo_ps[0:B, 0, 0, 0:D]
        c_ps = vo_ps[0:B, 0, 0, D:2 * D]

        block = ctx.enter_context(nc.Block())

        def batch_of(i, ahead):
            return i + ahead

        @block.sync
        def _(sp):
            def weight(dst, src, name):
                sp.dma_start(dst, src.rearrange("(t p) n -> p t n", p=P)).then_inc(ld[name], 16)

            sp.dma_start(cond_in[:], cond).then_inc(ld["cond"], 16)
            weight(we_in[:], Wul[D:2 * D, :], "we")
            weight(wp_in[:], Wp, "wp")
            weight(wq2_in[:], Wq2, "wq2")
            weight(wk2_in[:], Wk2, "wk2")
            weight(wu_in[:], Wul[0:D, :], "wu")
            for b in range(2):
                sp.dma_start(x_nat[:, b].rearrange("p t d -> p (t d)"), x_rows[b]).then_inc(x_loaded[b], 16)
            sp.dma_start(wv_in[:].rearrange("p h t n -> p (h t) n"), Wv.rearrange("(a p) n -> p a n", p=P)).then_inc(ld["wv"], 16)
            weight(wq1_in[:], Wq1, "wq1")
            weight(wk1_in[:], Wk1, "wk1")

            def load(j, slot):
                sp.wait_ge(xt_done, j - 1)
                sp.dma_start(x_nat[:, slot].rearrange("p t d -> p (t d)"), x_rows[j]).then_inc(x_loaded[slot], 16)

            def store(j, slot):
                sp.wait_ge(o_done, j + 1)
                sp.dma_start(out_rows[j], o_sb[:, slot].rearrange("p t d -> p (t d)")).then_inc(o_stored[slot], 16)

            load(2, 0)
            sp.wait_ge(row_made, 1)
            sp.dma_start(row_flat[:], row[:]).then_inc(row_moved, 16)
            load(3, 1)
            load(4, 0)
            store(0, 0)
            with sp.Fori(2, B - 4, 2) as i:
                for n in range(2):
                    load(i + (n + 3), (n + 1) % 2)
                    store(i + (n - 1), (n + 1) % 2)
            for i in range(B - 4, B):
                if i + 3 < B:
                    load(i + 3, (i + 1) % 2)
                store(i - 1, (i + 1) % 2)
            store(B - 1, 1)
            for slot in range(2):
                sp.wait_ge(o_stored[slot], 16 * (B // 2))

        @block.gpsimd
        def _(pool):
            for n, b in BIAS.items():
                pool.dma_start(bias_in[:, BROW[n], :], b.rearrange("(a n) -> a n", a=1)).then_inc(ld["bias"], 16)
            pool.dma_start(alpha_in[:], alpha.rearrange("(a n) -> a n", a=1).to_broadcast([B, 1])).then_inc(ld["alpha"], 16)
            nc.gpsimd.memset(ident[:], 0.0).then_inc(eye_zero, 1)
            nc.gpsimd.memset(eye[:], 0.0).then_inc(eye_zero, 1)
            nc.gpsimd.memset(ones[:], 1.0).then_inc(ones_made, 1)
            pool.wait_ge(eye_zero, 2)
            nc.gpsimd.affine_select(out=ident[:], in_=ident[:], compare_op=ALU.not_equal, fill=1.0,
                                    base=0, pattern=[[-1, P]], channel_multiplier=1).then_inc(eye_made, 1)
            nc.gpsimd.affine_select(out=eye[:], in_=eye[:], compare_op=ALU.not_equal, fill=1.0,
                                    base=0, pattern=[[P, DT], [-1, D]], channel_multiplier=1).then_inc(eye_made, 1)
            pool.wait_ge(row_moved, 16)
            for b in range(0, B, 8):
                nc.gpsimd.partition_broadcast(row_all[:, b:b + 8, :], row_flat[:, b:b + 8, :]).then_inc(row_spread, 1)

        @block.tensor
        def _(pe):
            mm = nc.tensor.matmul

            def weight_product(dst, lhs, rhs):
                for t in range(DT):
                    for c in range(DT):
                        last = mm(dst[:, t, :], lhs[:, c, t * P:(t + 1) * P], rhs[:, c, :], start=(c == 0), stop=(c == DT - 1))
                return last

            def vector_product(dst, w, vT, bias=None):
                for t in range(DT):
                    for c in range(DT):
                        last = mm(dst[:, t, :], w[:, c, t * P:(t + 1) * P], vT[:, c, :], start=(c == 0),
                                  stop=(c == DT - 1 and bias is None))
                    if bias is not None:
                        last = mm(dst[:, t, :], bias_in[0:1, BROW[bias], t * P:(t + 1) * P], ones[0:1, 0:B], start=False, stop=True)
                return last

            def row_product(dst, terms, bias=None):
                steps = [(vT[:, c, :], w[:, c, :]) for vT, w in terms for c in range(DT)]
                if bias is not None:
                    steps.append((ones[0:1, 0:B], bias_in[0:1, BROW[bias], :]))
                for n, (a, b) in enumerate(steps):
                    last = mm(dst, a, b, start=(n == 0), stop=(n == len(steps) - 1))
                return last

            def x_transpose(j, slot):
                for d in range(DT):
                    for s in range(ST):
                        last = nc.tensor.transpose(xt_ps[:, d, s * P:(s + 1) * P], x_nat[:, slot, s, d * P:(d + 1) * P], ident[:])
                last.then_inc(xt_done, 1)

            pe.wait_ge(eye_made, 1)
            pe.wait_ge(ld["cond"], 16)
            for c in range(DT):
                last = nc.tensor.transpose(condT_ps[:, c, :], cond_in[:, c * P:(c + 1) * P], ident[0:B, 0:B])
            last.then_inc(prep_pe["condT"], 1)
            pe.wait_ge(ld["we"], 16)
            for c in range(DT):
                for e in range(DT):
                    last = nc.tensor.transpose(wT_ps[:, c, e * P:(e + 1) * P], we_in[:, e, c * P:(c + 1) * P], ident[:])
            last.then_inc(prep_pe["wT"], 1)
            pe.wait_ge(prep_sb["condT"], 1)
            pe.wait_ge(ld["wp"], 16)
            pe.wait_ge(ones_made, 1)
            pe.wait_ge(ld["bias"], 16 * len(BIAS))
            vector_product(u_ps, wp_in, condT, "bp").then_inc(prep_pe["u"], 1)
            pe.wait_ge(prep_sb["wT"], 1)
            pe.wait_ge(ld["wq2"], 16)
            weight_product(g1_ps, wq2_in, wT).then_inc(prep_pe["g1"], 1)
            pe.wait_ge(ld["wk2"], 16)
            weight_product(g2_ps, wk2_in, wT).then_inc(prep_pe["g2"], 1)
            pe.wait_ge(prep_sb["u"], 1)
            pe.wait_ge(ld["wu"], 16)
            vector_product(rT_ps, wu_in, uT).then_inc(prep_pe["rT"], 1)
            pe.wait_ge(x_loaded[0], 16)
            x_transpose(0, 0)
            pe.wait_ge(prep_sb["rT"], 1)
            vector_product(a_ps, wq2_in, rT, "bq2").then_inc(prep_pe["a"], 1)
            pe.wait_ge(prep_sb["g1"], 1)
            pe.wait_ge(prep_sb["g2"], 1)
            weight_product(m_ps, g1T, g2T).then_inc(prep_pe["m"], 1)
            pe.wait_ge(prep_sb["a"], 1)
            vector_product(g_ps, g2T, aT).then_inc(prep_pe["g"], 1)
            pe.wait_ge(ld["wv"], 16)
            weight_product(z_ps, wT, wv_in[:, 1]).then_inc(prep_pe["z"], 1)
            pe.wait_ge(x_loaded[1], 16)
            pe.wait_ge(xl_done, 1)
            x_transpose(1, 1)
            row_product(rrow_ps, [(uT, wu_in)])
            row_product(c_ps, [(condT, wv_in[:, 0]), (rT, wv_in[:, 1])], "bv").then_inc(prep_pe["c"], 1)
            pe.wait_ge(ld["wq1"], 16)
            row_product(q1_ps, [(condT, wq1_in)], "bq1")
            pe.wait_ge(ld["wk1"], 16)
            row_product(k1_ps, [(condT, wk1_in)], "bk1").then_inc(prep_pe["k1"], 1)

            def split_product(dst, l_h, l_l, r_h, r_l, first=True):
                steps = [(l, r, c) for c in range(2) for l, r in ((l_h, r_h), (l_h, r_l), (l_l, r_h))]
                for n, (l, r, c) in enumerate(steps):
                    last = mm(dst, l(c), r(c), start=(first and n == 0), stop=(n == len(steps) - 1), skip_group_check=True)
                return last

            def queries(slot):
                for e in range(DT):
                    c0 = slice(e * P, (e + 1) * P)
                    last = split_product(t_ps[:, e, :], lambda c: m_h[:, c, c0], lambda c: m_l[:, c, c0],
                                         lambda c: x_h[:, slot, c, :], lambda c: x_l[:, slot, c, :])
                last.then_inc(t_done, 1)

            def scores(slot):
                for s in range(ST):
                    c0 = slice(s * P, (s + 1) * P)
                    last = split_product(s_ps[:, s, :], lambda c: t_h[:, c, c0], lambda c: t_l[:, c, c0],
                                         lambda c: x_h[:, slot, c, :], lambda c: x_l[:, slot, c, :])
                last.then_inc(s_done, 1)

            def values(slot, s):
                c0 = slice(s * P, (s + 1) * P)
                return split_product(vo_ps[:, slot, s, :], lambda c: x_h[:, slot, c, c0], lambda c: x_l[:, slot, c, c0],
                                     lambda c: zw_h[:, c, :], lambda c: zw_l[:, c, :])

            def mix(slot):
                for s in range(ST):
                    c0 = slice(s * P, (s + 1) * P)
                    last = split_product(vo_ps[:, slot, s, D:2 * D], lambda c: a_h[:, c, c0], lambda c: a_l[:, c, c0],
                                         lambda c: v_h[:, c, :], lambda c: v_l[:, c, :], first=False)
                last.then_inc(av_done, 1)

            def step(i, slot, skip=()):
                other = 1 - slot
                pe.wait_ge(tl_done, i + 1)
                scores(slot)
                if "o" not in skip:
                    pe.wait_ge(o_done, i - 1)
                values(slot, 0)
                if "t" not in skip:
                    pe.wait_ge(xl_done, i + 2)
                    queries(other)
                if "av" not in skip:
                    pe.wait_ge(vl_done, i)
                    pe.wait_ge(al_done, i)
                    mix(other)
                values(slot, 1).then_inc(v_done, 1)
                pe.wait_ge(a_done, i + 1)
                for k in range(ST):
                    for s in range(ST):
                        last = nc.tensor.transpose(at_ps[:, k, s * P:(s + 1) * P], a_nat[:, s, k * P:(k + 1) * P], ident[:])
                last.then_inc(at_done, 1)
                if "xt" not in skip:
                    pe.wait_ge(x_loaded[slot], (i - slot) * 8 + 32)
                    x_transpose(i + 2, slot)

            pe.wait_ge(prep_sb["mh"], 1)
            pe.wait_ge(prep_sb["ml"], 1)
            pe.wait_ge(xl_done, 1)
            queries(0)
            pe.wait_ge(a1_dve, 6)
            mm(ap_ps, ones[:, :], ap_diag[:], start=True, stop=True).then_inc(prep_pe["ap"], 1)
            pe.wait_ge(prep_sb["g"], 1)
            pe.wait_ge(prep_sb["apcol"], 1)
            pe.wait_ge(row_made, 1)
            for n in ("zh", "zl", "wh", "wl"):
                pe.wait_ge(prep_sb[n], 1)
            step(0, 0, ("o", "av"))
            step(1, 1, ("o",))
            with pe.Fori(2, B - 2, 2) as i:
                step(i, 0)
                step(i + 1, 1)
            step(B - 2, 0, ("xt",))
            step(B - 1, 1, ("xt", "t"))
            pe.wait_ge(vl_done, B)
            pe.wait_ge(al_done, B)
            mix(1)

        @block.scalar
        def _(act):
            copy = nc.scalar.copy

            act.wait_ge(prep_pe["condT"], 1)
            copy(condT[:], condT_ps).then_inc(prep_sb["condT"], 1)
            act.wait_ge(prep_pe["u"], 1)
            nc.scalar.activation(uT[:], u_ps, ACT.Gelu).then_inc(prep_sb["u"], 1)
            act.wait_ge(prep_pe["g2"], 1)
            copy(g2T[:], g2_ps).then_inc(prep_sb["g2"], 1)

            def x_high(slot):
                copy(x_h[:, slot], xt_ps[:]).then_inc(xh_done, 1)

            act.wait_ge(xt_done, 1)
            x_high(0)
            act.wait_ge(prep_pe["m"], 1)
            copy(m_h[:], m_ps[:]).then_inc(prep_sb["mh"], 1)
            act.wait_ge(prep_pe["z"], 1)
            copy(zw_h[:, :, 0:D], z_ps).then_inc(prep_sb["zh"], 1)
            act.wait_ge(prep_sb["wnat"], 1)
            copy(zw_h[:, :, D:2 * D], w_nat[:]).then_inc(prep_sb["wh"], 1)
            act.wait_ge(prep_pe["k1"], 1)
            copy(q1[:], q1_ps).then_inc(prep_sb["q1"], 1)

            def t_high(i):
                act.wait_ge(t_done, i + 1)
                for e in range(DT):
                    last = nc.scalar.activation(t_h[:, e, :], t_ps[:, e, :], ACT.Identity, bias=g_of(i, e))
                last.then_inc(th_done, 1)

            def g_of(i, e):
                return gT[:, i, e:e + 1]

            act.wait_ge(prep_sb["g"], 1)
            t_high(0)
            act.wait_ge(a1_dve, 2)
            nc.scalar.activation(a1[:, 2:3], a1[:, 0:1], ACT.Exp, bias=a1[:, 1:2], scale=SCALE).then_inc(a1_exp, 1)

            def step(i, slot, skip=()):
                if "a" not in skip:
                    act.wait_ge(at_done, i)
                    copy(a_h[:], at_ps[:]).then_inc(ah_done, 1)
                if "x" not in skip:
                    act.wait_ge(xt_done, i + 2)
                    x_high(1 - slot)
                if "a" not in skip:
                    act.wait_ge(v_done, i)
                    copy(v_h[:], vo_ps[:, 1 - slot, :, 0:D]).then_inc(vh_done, 1)
                act.wait_ge(max_done, i + 1)
                for s in range(ST):
                    last = nc.scalar.activation(e_nat[:, s, :], s_ps[:, s, :], ACT.Exp, bias=neg_max[:, s:s + 1],
                                                accum_out=den[:, s:s + 1])
                last.then_inc(e_done, 1)
                if "x" not in skip:
                    t_high(i + 1)

            step(0, 0, ("a",))
            step(1, 1)
            with act.Fori(2, B - 2, 2) as i:
                step(i, 0)
                step(i + 1, 1)
            step(B - 2, 0)
            step(B - 1, 1, ("x",))
            act.wait_ge(at_done, B)
            copy(a_h[:], at_ps[:]).then_inc(ah_done, 1)
            act.wait_ge(v_done, B)
            copy(v_h[:], vo_ps[:, 1, :, 0:D]).then_inc(vh_done, 1)

        @block.vector
        def _(dve):
            tt, ts, stt = nc.vector.tensor_tensor, nc.vector.tensor_scalar, nc.vector.scalar_tensor_tensor

            def low(dst, src, high):
                return tt(dst, src, high.bitcast(F32), ALU.subtract)

            def x_low(slot, n):
                dve.wait_ge(xh_done, n)
                low(x_l[:, slot], xt_ps[:], x_h[:, slot]).then_inc(xl_done, 1)

            dve.wait_ge(eye_made, 2)
            dve.wait_ge(prep_pe["wT"], 1)
            tt(wT[:], wT_ps, eye[:], ALU.add).then_inc(prep_sb["wT"], 1)
            tt(w_nat[:], we_in[:], eye[:], ALU.add).then_inc(prep_sb["wnat"], 1)
            dve.wait_ge(prep_pe["g1"], 1)
            ts(g1T[:], g1_ps, SCALE, None, ALU.mult).then_inc(prep_sb["g1"], 1)
            dve.wait_ge(prep_pe["rT"], 1)
            nc.vector.tensor_copy(rT[:], rT_ps).then_inc(prep_sb["rT"], 1)
            dve.wait_ge(prep_pe["a"], 1)
            ts(aT[:], a_ps, SCALE, None, ALU.mult).then_inc(prep_sb["a"], 1)
            x_low(0, 1)
            dve.wait_ge(prep_sb["mh"], 1)
            low(m_l[:], m_ps[:], m_h[:]).then_inc(prep_sb["ml"], 1)
            dve.wait_ge(prep_pe["g"], 1)
            nc.vector.tensor_copy(gT[:].rearrange("p b t -> p t b"), g_ps).then_inc(prep_sb["g"], 1)
            dve.wait_ge(prep_sb["zh"], 1)
            low(zw_l[:, :, 0:D], z_ps, zw_h[:, :, 0:D]).then_inc(prep_sb["zl"], 1)
            dve.wait_ge(prep_sb["wh"], 1)
            low(zw_l[:, :, D:2 * D], w_nat[:], zw_h[:, :, D:2 * D]).then_inc(prep_sb["wl"], 1)
            dve.wait_ge(prep_sb["q1"], 1)
            nc.vector.tensor_tensor_reduce(out=qk1[:], in0=q1[:], in1=k1_ps, scale=1.0, scalar=0.0, op0=ALU.mult,
                                           op1=ALU.add, accum_out=a1[:, 0:1]).then_inc(a1_dve, 1)
            dve.wait_ge(a1_dve, 1)
            ts(a1[:, 1:2], a1[:, 0:1], -SCALE, None, ALU.mult).then_inc(a1_dve, 1)
            dve.wait_ge(a1_exp, 1)
            ts(a1[:, 3:4], a1[:, 2:3], float(S), None, ALU.mult).then_inc(a1_dve, 1)
            dve.wait_ge(a1_dve, 3)
            nc.vector.reciprocal(a1[:, 4:5], a1[:, 3:4]).then_inc(a1_dve, 1)
            dve.wait_ge(a1_dve, 4)
            dve.wait_ge(ld["alpha"], 16)
            stt(out=a1[:, 5:6], in0=a1[:, 2:3], scalar=a1[:, 4:5], in1=alpha_in[:], op0=ALU.mult, op1=ALU.mult).then_inc(a1_dve, 1)
            dve.wait_ge(a1_dve, 5)
            ts(ap_diag[:], ident[0:B, 0:B], a1[:, 5:6], None, ALU.mult).then_inc(a1_dve, 1)
            ts(a1[:, 6:7], a1[:, 5:6], -float(S), 1.0, ALU.mult, ALU.add).then_inc(a1_dve, 1)
            dve.wait_ge(prep_pe["c"], 1)
            nc.vector.tensor_copy(r_row[:], rrow_ps).then_inc(prep_sb["rrow"], 1)
            dve.wait_ge(prep_sb["rrow"], 1)
            dve.wait_ge(a1_dve, 7)
            stt(out=row[:], in0=c_ps, scalar=a1[:, 6:7], in1=r_row[:], op0=ALU.mult, op1=ALU.add).then_inc(row_made, 1)
            dve.wait_ge(prep_pe["ap"], 1)
            nc.vector.tensor_copy(ap_col[:], ap_ps).then_inc(prep_sb["apcol"], 1)

            def t_low(i):
                dve.wait_ge(th_done, i + 1)
                for e in range(DT):
                    last = stt(out=t_l[:, e, :], in0=t_ps[:, e, :], scalar=gT[:, i, e:e + 1],
                               in1=t_h[:, e, :].bitcast(F32), op0=ALU.add, op1=ALU.subtract)
                last.then_inc(tl_done, 1)

            def output(j, slot, wait=True):
                dve.wait_ge(av_done, j + 1)
                if wait:
                    dve.wait_ge(o_stored[slot], (j - slot) * 8)
                for s in range(ST):
                    last = tt(o_sb[:, slot, s, :], vo_ps[:, slot, s, D:2 * D], row_of(j), ALU.add)
                last.then_inc(o_done, 1)

            def row_of(j):
                return row_all[:, j, :]

            t_low(0)
            dve.wait_ge(prep_sb["apcol"], 1)

            def step(i, slot, skip=()):
                if "a" not in skip:
                    dve.wait_ge(ah_done, i)
                    low(a_l[:], at_ps[:], a_h[:]).then_inc(al_done, 1)
                if "x" not in skip:
                    x_low(1 - slot, i + 2)
                dve.wait_ge(s_done, i + 1)
                nc.vector.tensor_reduce(neg_max[:], s_ps[:], AX.X, ALU.max, negate=True).then_inc(max_done, 1)
                if "a" not in skip:
                    dve.wait_ge(vh_done, i)
                    low(v_l[:], vo_ps[:, 1 - slot, :, 0:D], v_h[:]).then_inc(vl_done, 1)
                dve.wait_ge(e_done, i + 1)
                nc.vector.reciprocal(r_den[:], den[:]).then_inc(rden_done, 1)
                dve.wait_ge(rden_done, i + 1)
                for s in range(ST):
                    last = ts(a_nat[:, s, :], e_nat[:, s, :], r_den[:, s:s + 1], ap_col[:, i:i + 1] if isinstance(i, int) else ap_col[:, bass.ds(i, 1)],
                              ALU.mult, ALU.subtract)
                last.then_inc(a_done, 1)
                if "x" not in skip:
                    t_low(i + 1)
                if "a" not in skip:
                    output(i - 1, 1 - slot, "first" not in skip)

            step(0, 0, ("a",))
            dve.wait_ge(row_spread, B // 8)
            step(1, 1, ("first",))
            step(2, 0, ("first",))
            step(3, 1)
            with dve.Fori(4, B - 2, 2) as i:
                step(i, 0)
                step(i + 1, 1)
            step(B - 2, 0)
            step(B - 1, 1, ("x",))
            dve.wait_ge(ah_done, B)
            low(a_l[:], at_ps[:], a_h[:]).then_inc(al_done, 1)
            dve.wait_ge(vh_done, B)
            low(v_l[:], vo_ps[:, 1, :, 0:D], v_h[:]).then_inc(vl_done, 1)
            output(B - 1, 1)


_INS = ["x", "cond_1024", "L0_cond_weight_matrix", "L0_cond_W_proj", "L0_cond_b_proj", "L1_cond_Wq1", "L1_cond_bq1",
        "L1_cond_Wq2", "L1_cond_bq2", "L1_cond_Wk1", "L1_cond_bk1", "L1_cond_Wk2", "L1_cond_bk2", "L1_cond_Wv",
        "L1_cond_bv", "L1_cond_alpha"]


def kernel(**inputs):
    import numpy as _np
    import concourse.bacc as _bacc
    from concourse import mybir as _mybir
    from concourse.bass_utils import run_bass_kernel_spmd as _run

    nc = _bacc.Bacc("TRN2", target_bir_lowering=False, num_devices=1)
    arrays, args = {}, []
    for name in _INS:
        a = _np.ascontiguousarray(inputs[name])
        arrays[f"in_{name}"] = a
        args.append(nc.dram_tensor(f"in_{name}", a.shape, _mybir.dt.from_np(a.dtype), kind="ExternalInput").ap())
    out = nc.dram_tensor("out_0", arrays["in_x"].shape, _mybir.dt.float32, kind="ExternalOutput").ap()
    build(nc, *args, out)
    r = _run(nc, [arrays], core_ids=[0])
    return r.results[0]["out_0"]
```

```python
from contextlib import ExitStack

import concourse.bass as bass
from concourse import mybir

ALU = mybir.AluOpType
ACT = mybir.ActivationFunctionType
AX = mybir.AxisListType
F32 = mybir.dt.float32
F32R = mybir.dt.float32r
P = 128




def build(nc, x, cond, Wul, Wp, Wq1, Wq2, Wk1, Wk2, Wv, alpha, biases, out):
    B, S, D = x.shape
    DT = D // P
    ST = S // P
    SCALE = float(D) ** -0.5
    assert DT == 2 and ST == 2 and B % 2 == 0 and B >= 6
    BROW = {n: i for i, n in enumerate(("bp", "bq1", "bk1", "bq2", "bk2", "bv"))}

    x_rows = x.rearrange("b (p t) d -> b p (t d)", t=ST)
    out_rows = out.rearrange("b (p t) d -> b p (t d)", t=ST)

    with ExitStack() as ctx:
        def sb(name, shape, dt=F32):
            return ctx.enter_context(nc.sbuf_tensor(name, shape, dt))

        def ps(name, shape):
            return ctx.enter_context(nc.psum_tensor(name, shape, F32))

        def sem(name):
            return ctx.enter_context(nc.semaphore(name))

        we_in = sb("we_in", [P, DT, D])
        wu_in = sb("wu_in", [P, DT, D])
        wp_in = sb("wp_in", [P, DT, D])
        wq1_in = sb("wq1_in", [P, DT, D])
        wk1_in = sb("wk1_in", [P, DT, D])
        wq2_in = sb("wq2_in", [P, DT, D])
        wk2_in = sb("wk2_in", [P, DT, D])
        wv_in = sb("wv_in", [P, 2, DT, D])
        cond_in = sb("cond_in", [B, D])
        bias_in = sb("bias_in", [len(BROW), D])
        alpha_in = sb("alpha_in", [P, 1])
        ident = sb("ident", [P, P])
        eye = sb("eye", [P, DT, D])
        ones = sb("ones", [P, P])
        wT = sb("wT", [P, DT, D])
        w_nat = sb("w_nat", [P, DT, D])
        g1T = sb("g1T", [P, DT, D])
        g2T = sb("g2T", [P, DT, D])
        m_h = sb("m_h", [P, DT, D], F32R)
        m_l = sb("m_l", [P, DT, D], F32R)
        zw_h = sb("zw_h", [P, DT, 2 * D], F32R)
        zw_l = sb("zw_l", [P, DT, 2 * D], F32R)
        condT = sb("condT", [P, DT, B])
        warm = sb("warm", [P, 2])
        biasT = sb("biasT", [P, DT, len(BROW)])
        uT = sb("uT", [P, DT, B])
        rT = sb("rT", [P, DT, B])
        aT = sb("aT", [P, DT, B])
        kappaT = sb("kappaT", [P, DT, B])
        a_kappa = sb("a_kappa", [P, DT, B])
        gT = sb("gT", [P, B, DT])
        q1T = sb("q1T", [P, DT, B])
        q1_k1 = sb("q1_k1", [P, DT, B])
        cT = sb("cT", [P, DT, B])
        rowT = sb("rowT", [P, DT, B])
        w_row = sb("w_row", [B, D])
        row = sb("row", [B, D])
        rows_flat = sb("rows_flat", [33, B, D])
        row_all = sb("row_all", [P, B, D])
        w_all = sb("w_all", [P, B, D])
        a_kappa_col = sb("a_kappa_col", [P, B])
        a1_neg = sb("a1_neg", [P, B])
        a1_diff = sb("a1_diff", [P, B])
        a1_exp = sb("a1_exp", [P, B])
        a1_sum = sb("a1_sum", [P, B])
        a1_rec = sb("a1_rec", [P, B])
        alpha_p1 = sb("alpha_p1", [P, B])
        neg_alpha_p1 = sb("neg_alpha_p1", [P, B])
        a_row_sum = sb("a_row_sum", [P, B])
        x_nat = sb("x_nat", [P, 2, ST, D])
        x_h = sb("x_h", [P, 2, DT, S], F32R)
        x_l = sb("x_l", [P, 2, DT, S], F32R)
        t_h = sb("t_h", [P, DT, S], F32R)
        t_l = sb("t_l", [P, DT, S], F32R)
        v_h = sb("v_h", [P, ST, D], F32R)
        v_l = sb("v_l", [P, ST, D], F32R)
        x_w = sb("x_w", [P, ST, D])
        shift = sb("shift", [P, 2, ST])
        neg_max = sb("neg_max", [P, ST])
        neg_top = sb("neg_top", [P, ST])
        exp_bias = sb("exp_bias", [P, ST])
        e_nat = sb("e_nat", [P, ST, S])
        den = sb("den", [P, ST])
        r_den = sb("r_den", [P, ST])
        a_nat = sb("a_nat", [P, ST, S])
        a_h = sb("a_h", [P, ST, S], F32R)
        a_l = sb("a_l", [P, ST, S], F32R)
        o_sb = sb("o_sb", [P, 2, ST, D])

        xt_ps = ps("xt_ps", [P, DT, S])
        t_ps = ps("t_ps", [P, DT, S])
        s_ps = ps("s_ps", [P, ST, S])
        at_ps = ps("at_ps", [P, ST, S])
        vo_ps = ps("vo_ps", [P, 2, ST, 2 * D])

        ld = {n: sem("ld_" + n) for n in ("we", "wu", "wp", "wq1", "wk1", "wq2", "wk2", "wv", "cond", "bias", "alpha")}
        x_loaded = [sem("x_loaded0"), sem("x_loaded1")]
        eye_zero = sem("eye_zero")
        eye_made = sem("eye_made")
        ones_made = sem("ones_made")
        prep_pe = {n: sem("pe_" + n) for n in ("cond", "wT", "u", "rT", "g1", "g2", "a_kappa", "m", "z", "g", "w_row",
                                               "heads", "sums", "row")}
        prep_sb = {n: sem("sb_" + n) for n in ("cond", "wT", "wnat", "u", "rT", "g1", "g2", "a_kappa", "products", "mh", "ml",
                                               "zh", "zl", "wh", "wl", "g", "w_row", "q1", "heads", "a1_neg", "sums", "a1_exp",
                                               "a1_sum", "a1_rec", "alpha_p1", "p1_columns", "c_scaled", "rowT", "row")}
        w_moved = sem("w_moved")
        row_moved = sem("row_moved")
        w_spread = sem("w_spread")
        row_spread = sem("row_spread")
        xt_done, t_done, s_done, v_done, at_done, av_done = (sem(n) for n in ("xt_done", "t_done", "s_done", "v_done", "at_done", "av_done"))
        xh_done, th_done, e_done, a_done, vh_done, ah_done = (
            sem(n) for n in ("xh_done", "th_done", "e_done", "a_done", "vh_done", "ah_done"))
        xl_done, tl_done, shift_done, max_done, top_done, bias_done, rden_done, vl_done, al_done, o_done = (
            sem(n) for n in ("xl_done", "tl_done", "shift_done", "max_done", "top_done", "bias_done", "rden_done",
                             "vl_done", "al_done", "o_done"))
        o_stored = [sem("o_stored0"), sem("o_stored1")]

        wT_ps = vo_ps[:, 0, 0, :].rearrange("p (t n) -> p t n", t=DT)
        g1_ps = vo_ps[:, 0, 1, :].rearrange("p (t n) -> p t n", t=DT)
        g2_ps = vo_ps[:, 1, 0, :].rearrange("p (t n) -> p t n", t=DT)
        z_ps = vo_ps[:, 1, 1, :].rearrange("p (t n) -> p t n", t=DT)
        m_ps = t_ps

        def pieces(bank):
            flat = bank[:].rearrange("p t n -> p (t n)")
            return [flat[:, n:n + DT * B].rearrange("p (t b) -> p t b", t=DT) for n in range(0, flat.shape[1], DT * B)]

        u_ps, rT_ps, a_ps, kappa_ps, g_ps = pieces(s_ps)[:5]
        condT_ps, q1_ps, k1_ps, c_ps, sums_ps = pieces(at_ps)[:5]
        biasT_ps = pieces(at_ps)[5][:, :, 0:len(BROW)]
        w_ps = at_ps[0:B, 0, :]
        row_ps = at_ps[0:B, 0, :]

        def one(i):
            return slice(i, i + 1) if isinstance(i, int) else bass.ds(i, 1)

        def bias_of(name, t):
            return biasT[:, t, BROW[name]:BROW[name] + 1]

        block = ctx.enter_context(nc.Block())

        RUNS = [(0, 4), (4, 18), (18, B)]

        @block.sync
        def _(sp):
            def weight(dst, src, name):
                sp.dma_start(dst, src.rearrange("(t p) n -> p t n", p=P)).then_inc(ld[name], 16)

            weight(we_in[:], Wul[D:2 * D, :], "we")
            weight(wp_in[:], Wp, "wp")
            weight(wq2_in[:], Wq2, "wq2")
            weight(wk2_in[:], Wk2, "wk2")
            weight(wu_in[:], Wul[0:D, :], "wu")
            for b in range(2):
                sp.dma_start(x_nat[:, b].rearrange("p t d -> p (t d)"), x_rows[b]).then_inc(x_loaded[b], 16)
            sp.dma_start(wv_in[:].rearrange("p h t n -> p (h t) n"), Wv.rearrange("(a p) n -> p a n", p=P)).then_inc(ld["wv"], 16)
            weight(wq1_in[:], Wq1, "wq1")
            weight(wk1_in[:], Wk1, "wk1")

            def load(j, slot):
                sp.wait_ge(xt_done, j - 1)
                sp.wait_ge(shift_done, j - 1)
                sp.dma_start(x_nat[:, slot].rearrange("p t d -> p (t d)"), x_rows[j]).then_inc(x_loaded[slot], 16)

            def store(j, slot):
                sp.wait_ge(o_done, j + 1)
                sp.dma_start(out_rows[j], o_sb[:, slot].rearrange("p t d -> p (t d)")).then_inc(o_stored[slot], 16)

            sp.wait_ge(prep_sb["w_row"], 1)
            sp.dma_start(rows_flat[32:33], w_row[:]).then_inc(w_moved, 16)
            load(2, 0)
            sp.wait_ge(prep_sb["row"], 1)
            sp.dma_start(rows_flat[0:1], row[:]).then_inc(row_moved, 16)
            load(3, 1)
            load(4, 0)
            store(0, 0)
            with sp.Fori(2, B - 4, 2) as i:
                for n in range(2):
                    load(i + (n + 3), (n + 1) % 2)
                    store(i + (n - 1), (n + 1) % 2)
            for i in range(B - 4, B):
                if i + 3 < B:
                    load(i + 3, (i + 1) % 2)
                store(i - 1, (i + 1) % 2)
            store(B - 1, 1)
            for slot in range(2):
                sp.wait_ge(o_stored[slot], 16 * (B // 2))

        @block.gpsimd
        def _(pool):
            nc.gpsimd.memset(ident[:], 0.0).then_inc(eye_zero, 1)
            pool.wait_ge(eye_zero, 1)
            nc.gpsimd.affine_select(out=ident[:], in_=ident[:], compare_op=ALU.not_equal, fill=1.0,
                                    base=0, pattern=[[-1, P]], channel_multiplier=1).then_inc(eye_made, 1)
            nc.gpsimd.memset(eye[:], 0.0).then_inc(eye_zero, 1)
            pool.wait_ge(eye_zero, 2)
            nc.gpsimd.affine_select(out=eye[:], in_=eye[:], compare_op=ALU.not_equal, fill=1.0,
                                    base=0, pattern=[[P, DT], [-1, D]], channel_multiplier=1).then_inc(eye_made, 1)
            nc.gpsimd.memset(ones[:], 1.0).then_inc(ones_made, 1)
            pool.wait_ge(w_moved, 16)
            for b0, b1 in RUNS:
                nc.gpsimd.partition_broadcast(w_all[:, b0:b1, :], rows_flat[32:33, b0:b1, :]).then_inc(w_spread, 1)
            pool.wait_ge(row_moved, 16)
            for b0, b1 in RUNS:
                nc.gpsimd.partition_broadcast(row_all[:, b0:b1, :], rows_flat[0:1, b0:b1, :]).then_inc(row_spread, 1)

        @block.tensor
        def _(pe):
            mm = nc.tensor.matmul

            def weight_product(dst, lhs, rhs):
                for t in range(DT):
                    for c in range(DT):
                        last = mm(dst[:, t, :], lhs[:, c, t * P:(t + 1) * P], rhs[:, c, :], start=(c == 0), stop=(c == DT - 1))
                return last

            def vector_product(dst, terms):
                for t in range(DT):
                    steps = [(w[:, c, t * P:(t + 1) * P], vT[:, c, :]) for w, vT in terms for c in range(DT)]
                    for n, (w, vT) in enumerate(steps):
                        last = mm(dst[:, t, :], w, vT, start=(n == 0), stop=(n == len(steps) - 1))
                return last

            def x_transpose(j, slot):
                for d in range(DT):
                    for s in range(ST):
                        last = nc.tensor.transpose(xt_ps[:, d, s * P:(s + 1) * P], x_nat[:, slot, s, d * P:(d + 1) * P], ident[:])
                last.then_inc(xt_done, 1)

            pe.wait_ge(eye_made, 1)
            pe.wait_ge(ld["cond"], 16)
            for c in range(DT):
                nc.tensor.transpose(condT_ps[:, c, :], cond_in[:, c * P:(c + 1) * P], ident[0:B, 0:B])
            pe.wait_ge(ld["bias"], 16)
            for c in range(DT):
                last = nc.tensor.transpose(biasT_ps[:, c, :], bias_in[:, c * P:(c + 1) * P], ident[0:len(BROW), 0:len(BROW)])
            last.then_inc(prep_pe["cond"], 1)
            pe.wait_ge(ld["we"], 16)
            for c in range(DT):
                for e in range(DT):
                    last = nc.tensor.transpose(wT_ps[:, c, e * P:(e + 1) * P], we_in[:, e, c * P:(c + 1) * P], ident[:])
            last.then_inc(prep_pe["wT"], 1)
            pe.wait_ge(prep_sb["cond"], 1)
            pe.wait_ge(ld["wp"], 16)
            vector_product(u_ps, [(wp_in, condT)]).then_inc(prep_pe["u"], 1)
            pe.wait_ge(prep_sb["wT"], 1)
            pe.wait_ge(ld["wq2"], 16)
            weight_product(g1_ps, wq2_in, wT).then_inc(prep_pe["g1"], 1)
            pe.wait_ge(prep_sb["u"], 1)
            pe.wait_ge(ld["wu"], 16)
            vector_product(rT_ps, [(wu_in, uT)]).then_inc(prep_pe["rT"], 1)
            pe.wait_ge(ld["wk2"], 16)
            weight_product(g2_ps, wk2_in, wT).then_inc(prep_pe["g2"], 1)
            pe.wait_ge(x_loaded[0], 16)
            x_transpose(0, 0)
            pe.wait_ge(prep_sb["rT"], 1)
            vector_product(a_ps, [(wq2_in, rT)])
            vector_product(kappa_ps, [(wk2_in, rT)]).then_inc(prep_pe["a_kappa"], 1)
            pe.wait_ge(prep_sb["g1"], 1)
            pe.wait_ge(prep_sb["g2"], 1)
            weight_product(m_ps, g1T, g2T).then_inc(prep_pe["m"], 1)
            pe.wait_ge(prep_sb["a_kappa"], 1)
            for c in range(DT):
                last = mm(w_ps, kappaT[:, c, :], g1T[:, c, :], start=(c == 0), stop=(c == DT - 1))
            last.then_inc(prep_pe["w_row"], 1)
            vector_product(g_ps, [(g2T, aT)]).then_inc(prep_pe["g"], 1)
            def split_product(dst, l_h, l_l, r_h, r_l, first=True):
                steps = [(l, r, c) for c in range(2) for l, r in ((l_h, r_h), (l_h, r_l), (l_l, r_h))]
                for n, (l, r, c) in enumerate(steps):
                    last = mm(dst, l(c), r(c), start=(first and n == 0), stop=(n == len(steps) - 1), skip_group_check=True)
                return last

            def queries(slot):
                for e in range(DT):
                    c0 = slice(e * P, (e + 1) * P)
                    last = split_product(t_ps[:, e, :], lambda c: m_h[:, c, c0], lambda c: m_l[:, c, c0],
                                         lambda c: x_h[:, slot, c, :], lambda c: x_l[:, slot, c, :])
                last.then_inc(t_done, 1)

            def scores(slot):
                for s in range(ST):
                    c0 = slice(s * P, (s + 1) * P)
                    last = split_product(s_ps[:, s, :], lambda c: t_h[:, c, c0], lambda c: t_l[:, c, c0],
                                         lambda c: x_h[:, slot, c, :], lambda c: x_l[:, slot, c, :])
                last.then_inc(s_done, 1)

            def values(slot, s):
                c0 = slice(s * P, (s + 1) * P)
                return split_product(vo_ps[:, slot, s, :], lambda c: x_h[:, slot, c, c0], lambda c: x_l[:, slot, c, c0],
                                     lambda c: zw_h[:, c, :], lambda c: zw_l[:, c, :])

            def mix(slot):
                for s in range(ST):
                    c0 = slice(s * P, (s + 1) * P)
                    last = split_product(vo_ps[:, slot, s, D:2 * D], lambda c: a_h[:, c, c0], lambda c: a_l[:, c, c0],
                                         lambda c: v_h[:, c, :], lambda c: v_l[:, c, :], first=False)
                last.then_inc(av_done, 1)

            def a_transpose():
                for k in range(ST):
                    for s in range(ST):
                        last = nc.tensor.transpose(at_ps[:, k, s * P:(s + 1) * P], a_nat[:, s, k * P:(k + 1) * P], ident[:])
                last.then_inc(at_done, 1)

            def step(i, slot, but=()):
                other = 1 - slot
                pe.wait_ge(tl_done, i + 1)
                scores(slot)
                if "o" not in but:
                    pe.wait_ge(o_done, i - 1)
                values(slot, 0)
                if "t" not in but:
                    pe.wait_ge(xl_done, i + 2)
                    queries(other)
                pe.wait_ge(vl_done, i)
                pe.wait_ge(al_done, i)
                mix(other)
                values(slot, 1).then_inc(v_done, 1)
                pe.wait_ge(a_done, i + 1)
                a_transpose()
                if "xt" not in but:
                    pe.wait_ge(x_loaded[slot], (i - slot) * 8 + 32)
                    x_transpose(i + 2, slot)

            pe.wait_ge(prep_sb["mh"], 1)
            pe.wait_ge(prep_sb["ml"], 1)
            pe.wait_ge(xl_done, 1)
            queries(0)
            pe.wait_ge(x_loaded[1], 16)
            x_transpose(1, 1)
            pe.wait_ge(ld["wv"], 16)
            weight_product(z_ps, wT, wv_in[:, 1]).then_inc(prep_pe["z"], 1)

            pe.wait_ge(prep_sb["g"], 1)
            pe.wait_ge(tl_done, 1)
            scores(0)
            pe.wait_ge(prep_sb["w_row"], 1)
            pe.wait_ge(ld["wq1"], 16)
            vector_product(q1_ps, [(wq1_in, condT)])
            pe.wait_ge(ld["wk1"], 16)
            vector_product(k1_ps, [(wk1_in, condT)])
            vector_product(c_ps, [(wv_in[:, 0], condT), (wv_in[:, 1], rT)]).then_inc(prep_pe["heads"], 1)
            pe.wait_ge(ones_made, 1)
            pe.wait_ge(prep_sb["products"], 1)
            pe.wait_ge(prep_sb["heads"], 1)
            for n, products in enumerate((a_kappa, q1_k1)):
                for c in range(DT):
                    last = mm(sums_ps[:, n, :], ones[:], products[:, c, :], start=(c == 0), stop=(c == DT - 1))
            last.then_inc(prep_pe["sums"], 1)
            for n in ("zh", "zl", "wh", "wl"):
                pe.wait_ge(prep_sb[n], 1)
            values(0, 0)
            pe.wait_ge(xl_done, 2)
            queries(1)
            values(0, 1).then_inc(v_done, 1)
            pe.wait_ge(prep_sb["rowT"], 1)
            for c in range(DT):
                last = nc.tensor.transpose(row_ps[:, c * P:(c + 1) * P], rowT[:, c, :], ident[:])
            last.then_inc(prep_pe["row"], 1)
            pe.wait_ge(prep_sb["row"], 1)
            pe.wait_ge(a_done, 1)
            a_transpose()
            pe.wait_ge(x_loaded[0], 32)
            x_transpose(2, 0)

            step(1, 1, ("o",))
            with pe.Fori(2, B - 2, 2) as i:
                step(i, 0)
                step(i + 1, 1)
            step(B - 2, 0, ("xt",))
            step(B - 1, 1, ("xt", "t"))
            pe.wait_ge(vl_done, B)
            pe.wait_ge(al_done, B)
            mix(1)

        @block.scalar
        def _(act):
            copy, activation = nc.scalar.copy, nc.scalar.activation

            act.dma_start(cond_in[:], cond).then_inc(ld["cond"], 16)
            act.dma_start(bias_in[:], biases).then_inc(ld["bias"], 16)
            act.dma_start(alpha_in[:], alpha.rearrange("(a n) -> a n", a=1).to_broadcast([P, 1])).then_inc(ld["alpha"], 16)
            act.wait_ge(eye_made, 1)
            activation(warm[:, 0:1], ident[:, 0:1], ACT.Gelu)
            act.wait_ge(prep_pe["cond"], 1)
            copy(biasT[:], biasT_ps)
            copy(condT[:], condT_ps).then_inc(prep_sb["cond"], 1)
            act.wait_ge(prep_pe["u"], 1)
            act.wait_ge(prep_sb["cond"], 1)
            for t in range(DT):
                last = activation(uT[:, t, :], u_ps[:, t, :], ACT.Gelu, bias=bias_of("bp", t))
            last.then_inc(prep_sb["u"], 1)
            activation(warm[:, 1:2], ident[:, 0:1], ACT.Exp)
            act.wait_ge(prep_sb["wnat"], 1)
            copy(zw_h[:, :, D:2 * D], w_nat[:]).then_inc(prep_sb["wh"], 1)
            act.wait_ge(prep_pe["g2"], 1)
            copy(g2T[:], g2_ps).then_inc(prep_sb["g2"], 1)

            def x_high(slot):
                copy(x_h[:, slot], xt_ps[:]).then_inc(xh_done, 1)

            def t_high(i):
                act.wait_ge(t_done, i + 1)
                for e in range(DT):
                    last = activation(t_h[:, e, :], t_ps[:, e, :], ACT.Identity, bias=gT[:, i, e:e + 1])
                last.then_inc(th_done, 1)

            def exponent(i):
                act.wait_ge(bias_done, i + 1)
                for s in range(ST):
                    last = activation(e_nat[:, s, :], s_ps[:, s, :], ACT.Exp, bias=exp_bias[:, s:s + 1],
                                      accum_out=den[:, s:s + 1])
                last.then_inc(e_done, 1)

            def normalise(i):
                act.wait_ge(rden_done, i + 1)
                for s in range(ST):
                    last = activation(a_nat[:, s, :], e_nat[:, s, :], ACT.Identity, bias=neg_alpha_p1[:, one(i)],
                                      scale=r_den[:, s:s + 1])
                last.then_inc(a_done, 1)

            act.wait_ge(xt_done, 1)
            x_high(0)
            act.wait_ge(prep_pe["m"], 1)
            copy(m_h[:], m_ps[:]).then_inc(prep_sb["mh"], 1)
            act.wait_ge(prep_pe["w_row"], 1)
            copy(w_row[:], w_ps).then_inc(prep_sb["w_row"], 1)
            act.wait_ge(prep_sb["g"], 1)
            t_high(0)
            act.wait_ge(xt_done, 2)
            x_high(1)
            act.wait_ge(prep_pe["z"], 1)
            copy(zw_h[:, :, 0:D], z_ps).then_inc(prep_sb["zh"], 1)
            act.wait_ge(prep_sb["sums"], 1)
            activation(a1_exp[:], a1_diff[:], ACT.Exp).then_inc(prep_sb["a1_exp"], 1)
            exponent(0)
            act.wait_ge(prep_sb["p1_columns"], 1)
            normalise(0)
            t_high(1)

            def step(i, slot, but=()):
                act.wait_ge(at_done, i)
                copy(a_h[:], at_ps[:]).then_inc(ah_done, 1)
                if "x" not in but:
                    act.wait_ge(xt_done, i + 2)
                    x_high(1 - slot)
                act.wait_ge(v_done, i)
                copy(v_h[:], vo_ps[:, 1 - slot, :, 0:D]).then_inc(vh_done, 1)
                exponent(i)
                normalise(i)
                if "x" not in but:
                    t_high(i + 1)

            step(1, 1)
            with act.Fori(2, B - 2, 2) as i:
                step(i, 0)
                step(i + 1, 1)
            step(B - 2, 0)
            step(B - 1, 1, ("x",))
            act.wait_ge(at_done, B)
            copy(a_h[:], at_ps[:]).then_inc(ah_done, 1)
            act.wait_ge(v_done, B)
            copy(v_h[:], vo_ps[:, 1, :, 0:D]).then_inc(vh_done, 1)

        @block.vector
        def _(dve):
            tt, ts, stt = nc.vector.tensor_tensor, nc.vector.tensor_scalar, nc.vector.scalar_tensor_tensor

            def low(dst, src, high):
                return tt(dst, src, high.bitcast(F32), ALU.subtract)

            def x_low(i, slot):
                dve.wait_ge(xh_done, i + 1)
                low(x_l[:, slot], xt_ps[:], x_h[:, slot]).then_inc(xl_done, 1)

            def t_low(i):
                dve.wait_ge(th_done, i + 1)
                for e in range(DT):
                    last = stt(out=t_l[:, e, :], in0=t_ps[:, e, :], scalar=gT[:, i, e:e + 1],
                               in1=t_h[:, e, :].bitcast(F32), op0=ALU.add, op1=ALU.subtract)
                last.then_inc(tl_done, 1)

            def a_low(i):
                dve.wait_ge(ah_done, i + 1)
                low(a_l[:], at_ps[:], a_h[:]).then_inc(al_done, 1)

            def v_low(i, slot):
                dve.wait_ge(vh_done, i + 1)
                low(v_l[:], vo_ps[:, slot, :, 0:D], v_h[:]).then_inc(vl_done, 1)

            def shifts(i, slot):
                dve.wait_ge(x_loaded[slot], (i - slot) * 8 + 16)
                for s in range(ST):
                    last = stt(out=x_w[:, s, :], in0=x_nat[:, slot, s, :], scalar=1.0, in1=w_all[:, one(i), :].rearrange("p o n -> p (o n)"),
                               op0=ALU.mult, op1=ALU.mult, accum_out=shift[:, slot, s:s + 1])
                last.then_inc(shift_done, 1)

            def maximum(i):
                dve.wait_ge(s_done, i + 1)
                nc.vector.tensor_reduce(neg_max[:], s_ps[:], AX.X, ALU.max, negate=True).then_inc(max_done, 1)

            def exponent_bias(i, slot):
                dve.wait_ge(shift_done, i + 1)
                dve.wait_ge(max_done, i + 1)
                stt(out=neg_top[:], in0=neg_max[:], scalar=a_kappa_col[:, one(i)], in1=shift[:, slot, :],
                    op0=ALU.subtract, op1=ALU.subtract).then_inc(top_done, 1)
                dve.wait_ge(top_done, i + 1)
                stt(out=exp_bias[:], in0=neg_top[:], scalar=a_kappa_col[:, one(i)], in1=shift[:, slot, :],
                    op0=ALU.add, op1=ALU.add).then_inc(bias_done, 1)

            def denominator(i):
                dve.wait_ge(e_done, i + 1)
                nc.vector.reciprocal(r_den[:], den[:]).then_inc(rden_done, 1)

            def output(j, slot, wait=True):
                dve.wait_ge(av_done, j + 1)
                if wait:
                    dve.wait_ge(o_stored[slot], (j - slot) * 8)
                tt(o_sb[:, slot], vo_ps[:, slot, :, D:2 * D], row_all[:, one(j), :].to_broadcast([P, ST, D]),
                   ALU.add).then_inc(o_done, 1)

            dve.wait_ge(eye_made, 2)
            dve.wait_ge(prep_pe["wT"], 1)
            tt(wT[:], wT_ps, eye[:], ALU.add).then_inc(prep_sb["wT"], 1)
            tt(w_nat[:], we_in[:], eye[:], ALU.add).then_inc(prep_sb["wnat"], 1)
            dve.wait_ge(prep_pe["g1"], 1)
            ts(g1T[:], g1_ps, SCALE, None, ALU.mult).then_inc(prep_sb["g1"], 1)
            dve.wait_ge(prep_pe["rT"], 1)
            nc.vector.tensor_copy(rT[:], rT_ps).then_inc(prep_sb["rT"], 1)
            dve.wait_ge(prep_sb["wh"], 1)
            low(zw_l[:, :, D:2 * D], w_nat[:], zw_h[:, :, D:2 * D]).then_inc(prep_sb["wl"], 1)
            dve.wait_ge(prep_pe["a_kappa"], 1)
            dve.wait_ge(prep_sb["cond"], 1)
            for t in range(DT):
                ts(aT[:, t, :], a_ps[:, t, :], bias_of("bq2", t), SCALE, ALU.add, ALU.mult)
                last = ts(kappaT[:, t, :], kappa_ps[:, t, :], bias_of("bk2", t), None, ALU.add)
            last.then_inc(prep_sb["a_kappa"], 1)
            x_low(0, 0)
            dve.wait_ge(prep_sb["a_kappa"], 1)
            tt(a_kappa[:], aT[:], kappaT[:], ALU.mult).then_inc(prep_sb["products"], 1)
            dve.wait_ge(prep_sb["mh"], 1)
            low(m_l[:], m_ps[:], m_h[:]).then_inc(prep_sb["ml"], 1)
            dve.wait_ge(prep_pe["g"], 1)
            nc.vector.tensor_copy(gT[:].rearrange("p b t -> p t b"), g_ps).then_inc(prep_sb["g"], 1)
            t_low(0)
            x_low(1, 1)
            dve.wait_ge(prep_sb["zh"], 1)
            low(zw_l[:, :, 0:D], z_ps, zw_h[:, :, 0:D]).then_inc(prep_sb["zl"], 1)
            dve.wait_ge(w_spread, 1)
            shifts(0, 0)
            maximum(0)
            dve.wait_ge(prep_pe["heads"], 1)
            for t in range(DT):
                last = ts(q1T[:, t, :], q1_ps[:, t, :], bias_of("bq1", t), None, ALU.add)
            last.then_inc(prep_sb["q1"], 1)
            for t in range(DT):
                ts(cT[:, t, :], c_ps[:, t, :], bias_of("bv", t), None, ALU.add)
            dve.wait_ge(prep_sb["q1"], 1)
            for t in range(DT):
                last = stt(out=q1_k1[:, t, :], in0=k1_ps[:, t, :], scalar=bias_of("bk1", t), in1=q1T[:, t, :],
                           op0=ALU.add, op1=ALU.mult)
            last.then_inc(prep_sb["heads"], 1)
            dve.wait_ge(prep_pe["sums"], 1)
            nc.vector.tensor_copy(a_kappa_col[:], sums_ps[:, 0, :])
            ts(a1_neg[:], sums_ps[:, 1, :], -SCALE, None, ALU.mult).then_inc(prep_sb["a1_neg"], 1)
            dve.wait_ge(prep_sb["a1_neg"], 1)
            stt(out=a1_diff[:], in0=sums_ps[:, 1, :], scalar=SCALE, in1=a1_neg[:], op0=ALU.mult, op1=ALU.add)\
                .then_inc(prep_sb["sums"], 1)
            exponent_bias(0, 0)
            dve.wait_ge(prep_sb["a1_exp"], 1)
            ts(a1_sum[:], a1_exp[:], float(S), None, ALU.mult).then_inc(prep_sb["a1_sum"], 1)
            dve.wait_ge(prep_sb["a1_sum"], 1)
            nc.vector.reciprocal(a1_rec[:], a1_sum[:]).then_inc(prep_sb["a1_rec"], 1)
            dve.wait_ge(prep_sb["a1_rec"], 1)
            dve.wait_ge(ld["alpha"], 16)
            stt(out=alpha_p1[:], in0=a1_exp[:], scalar=alpha_in[:], in1=a1_rec[:], op0=ALU.mult, op1=ALU.mult)\
                .then_inc(prep_sb["alpha_p1"], 1)
            dve.wait_ge(prep_sb["alpha_p1"], 1)
            ts(neg_alpha_p1[:], alpha_p1[:], -1.0, None, ALU.mult)
            ts(a_row_sum[:], alpha_p1[:], -float(S), 1.0, ALU.mult, ALU.add).then_inc(prep_sb["p1_columns"], 1)
            denominator(0)
            dve.wait_ge(prep_sb["p1_columns"], 1)
            for t in range(DT):
                last = tt(cT[:, t, :], cT[:, t, :], a_row_sum[:], ALU.mult)
            last.then_inc(prep_sb["c_scaled"], 1)
            dve.wait_ge(prep_sb["c_scaled"], 1)
            tt(rowT[:], cT[:], rT[:], ALU.add).then_inc(prep_sb["rowT"], 1)
            dve.wait_ge(prep_pe["row"], 1)
            nc.vector.tensor_copy(row[:], row_ps).then_inc(prep_sb["row"], 1)
            t_low(1)
            shifts(1, 1)

            def step(i, slot, but=()):
                a_low(i - 1)
                if "x" not in but:
                    x_low(i + 1, 1 - slot)
                maximum(i)
                exponent_bias(i, slot)
                v_low(i - 1, 1 - slot)
                denominator(i)
                if "x" not in but:
                    shifts(i + 1, 1 - slot)
                if "row" in but:
                    dve.wait_ge(row_spread, 1)
                output(i - 1, 1 - slot, "first" not in but)
                if "x" not in but:
                    t_low(i + 1)

            step(1, 1, ("first", "row"))
            step(2, 0, ("first",))
            dve.wait_ge(w_spread, len(RUNS))
            step(3, 1)
            dve.wait_ge(row_spread, len(RUNS))
            with dve.Fori(4, B - 2, 2) as i:
                step(i, 0)
                step(i + 1, 1)
            step(B - 2, 0)
            step(B - 1, 1, ("x",))
            a_low(B - 1)
            v_low(B - 1, 1)
            output(B - 1, 1)


_INS = ["x", "cond_1024", "L0_cond_weight_matrix", "L0_cond_W_proj", "L1_cond_Wq1", "L1_cond_Wq2", "L1_cond_Wk1",
        "L1_cond_Wk2", "L1_cond_Wv", "L1_cond_alpha"]
_BIASES = ["L0_cond_b_proj", "L1_cond_bq1", "L1_cond_bk1", "L1_cond_bq2", "L1_cond_bk2", "L1_cond_bv"]


def kernel(**inputs):
    import numpy as _np
    import concourse.bacc as _bacc
    from concourse import mybir as _mybir
    from concourse.bass_utils import run_bass_kernel_spmd as _run

    nc = _bacc.Bacc("TRN2", target_bir_lowering=False, num_devices=1)
    arrays, args = {}, []
    laid_out = {name: inputs[name] for name in _INS}
    laid_out["biases"] = _np.stack([_np.asarray(inputs[name]) for name in _BIASES])
    for name, a in laid_out.items():
        a = _np.ascontiguousarray(a)
        arrays[f"in_{name}"] = a
        args.append(nc.dram_tensor(f"in_{name}", a.shape, _mybir.dt.from_np(a.dtype), kind="ExternalInput").ap())
    out = nc.dram_tensor("out_0", arrays["in_x"].shape, _mybir.dt.float32, kind="ExternalOutput").ap()
    build(nc, *args, out)
    r = _run(nc, [arrays], core_ids=[0])
    return r.results[0]["out_0"]
```

```python
from contextlib import ExitStack

import concourse.bass as bass
from concourse import mybir

ALU = mybir.AluOpType
ACT = mybir.ActivationFunctionType
AX = mybir.AxisListType
F32 = mybir.dt.float32
F32R = mybir.dt.float32r
P = 128




def build(nc, x, Wul, Wp, Wq1, Wq2, Wk1, Wk2, Wv, alpha, x_columns, we_columns, cond_columns, bias_columns, out):
    B, S, D = x.shape
    DT = D // P
    ST = S // P
    SCALE = float(D) ** -0.5
    assert DT == 2 and ST == 2 and B % 2 == 0 and B >= 6
    BROW = {n: i for i, n in enumerate(("bp", "bq1", "bk1", "bq2", "bk2", "bv"))}

    x_rows = x.rearrange("b (p t) d -> b p (t d)", t=ST)
    out_rows = out.rearrange("b (p t) d -> b p (t d)", t=ST)

    with ExitStack() as ctx:
        def sb(name, shape, dt=F32):
            return ctx.enter_context(nc.sbuf_tensor(name, shape, dt))

        def ps(name, shape):
            return ctx.enter_context(nc.psum_tensor(name, shape, F32))

        def sem(name):
            return ctx.enter_context(nc.semaphore(name))

        we_in = sb("we_in", [P, DT, D])
        wu_in = sb("wu_in", [P, DT, D])
        wp_in = sb("wp_in", [P, DT, D])
        wq1_in = sb("wq1_in", [P, DT, D])
        wk1_in = sb("wk1_in", [P, DT, D])
        wq2_in = sb("wq2_in", [P, DT, D])
        wk2_in = sb("wk2_in", [P, DT, D])
        wv_in = sb("wv_in", [P, 2, DT, D])
        weT_in = sb("weT_in", [P, DT, D])
        alpha_in = sb("alpha_in", [P, 1])
        ident = sb("ident", [P, P])
        eye = sb("eye", [P, DT, D])
        ones = sb("ones", [P, P])
        zeros = sb("zeros", [P, DT, S])
        wT = sb("wT", [P, DT, D])
        w_nat = sb("w_nat", [P, DT, D])
        g1T = sb("g1T", [P, DT, D])
        g2T = sb("g2T", [P, DT, D])
        m_h = sb("m_h", [P, DT, D], F32R)
        m_l = sb("m_l", [P, DT, D], F32R)
        zw_h = sb("zw_h", [P, DT, 2 * D], F32R)
        zw_l = sb("zw_l", [P, DT, 2 * D], F32R)
        condT = sb("condT", [P, DT, B])
        warm = sb("warm", [P, 2])
        biasT = sb("biasT", [P, DT, len(BROW)])
        uT = sb("uT", [P, DT, B])
        rT = sb("rT", [P, DT, B])
        aT = sb("aT", [P, DT, B])
        kappaT = sb("kappaT", [P, DT, B])
        a_kappa = sb("a_kappa", [P, DT, B])
        gT = sb("gT", [P, B, DT])
        q1T = sb("q1T", [P, DT, B])
        q1_k1 = sb("q1_k1", [P, DT, B])
        cT = sb("cT", [P, DT, B])
        rowT = sb("rowT", [P, DT, B])
        w_row = sb("w_row", [B, D])
        row = sb("row", [B, D])
        rows_flat = sb("rows_flat", [33, B, D])
        row_all = sb("row_all", [P, B, D])
        w_all = sb("w_all", [P, B, D])
        a_kappa_col = sb("a_kappa_col", [P, B])
        a1_neg = sb("a1_neg", [P, B])
        a1_diff = sb("a1_diff", [P, B])
        a1_exp = sb("a1_exp", [P, B])
        a1_sum = sb("a1_sum", [P, B])
        a1_rec = sb("a1_rec", [P, B])
        alpha_p1 = sb("alpha_p1", [P, B])
        neg_alpha_p1 = sb("neg_alpha_p1", [P, B])
        a_row_sum = sb("a_row_sum", [P, B])
        x_nat = sb("x_nat", [P, 2, ST, D])
        x_col = sb("x_col", [P, 2, DT, S])
        x_h = sb("x_h", [P, 2, DT, S], F32R)
        x_l = sb("x_l", [P, 2, DT, S], F32R)
        t_h = sb("t_h", [P, DT, S], F32R)
        t_l = sb("t_l", [P, DT, S], F32R)
        v_h = sb("v_h", [P, ST, D], F32R)
        v_l = sb("v_l", [P, ST, D], F32R)
        x_w = sb("x_w", [P, ST, D])
        shift = sb("shift", [P, 2, ST])
        neg_max = sb("neg_max", [P, ST])
        neg_top = sb("neg_top", [P, ST])
        exp_bias = sb("exp_bias", [P, ST])
        e_nat = sb("e_nat", [P, ST, S])
        den = sb("den", [P, ST])
        r_den = sb("r_den", [P, ST])
        a_nat = sb("a_nat", [P, ST, S])
        a_h = sb("a_h", [P, ST, S], F32R)
        a_l = sb("a_l", [P, ST, S], F32R)
        o_sb = sb("o_sb", [P, 2, ST, D])

        t_ps = ps("t_ps", [P, DT, 2 * S])
        s_ps = ps("s_ps", [P, ST, S])
        at_ps = ps("at_ps", [P, ST, S])
        vo_ps = ps("vo_ps", [P, 2, ST, 2 * D])

        tail_ps = (at_ps[:].rearrange("p k q -> p (k q)")[:, 0:S].rearrange("p (k q) -> p k q", k=ST),
                   t_ps[:, 0, 0:S].rearrange("p (k q) -> p k q", k=ST))

        v_last_h, v_last_l = x_h[:, 0], x_l[:, 0]

        ld = {n: sem("ld_" + n) for n in ("we", "weT", "wu", "wp", "wq1", "wk1", "wq2", "wk2", "wv", "cond", "bias", "alpha")}
        x_loaded = [sem("x_loaded0"), sem("x_loaded1")]
        xc_loaded = [sem("xc_loaded0"), sem("xc_loaded1")]
        eye_zero = sem("eye_zero")
        eye_made = sem("eye_made")
        ones_made = sem("ones_made")
        zeros_made = sem("zeros_made")
        prep_pe = {n: sem("pe_" + n) for n in ("u", "rT", "g1", "g2", "a_kappa", "m", "z", "g", "w_row",
                                               "heads", "sums", "c", "row")}
        prep_sb = {n: sem("sb_" + n) for n in ("wT", "wnat", "u", "rT", "g1", "g2", "a_kappa", "products", "mh", "ml",
                                               "zh", "zl", "wh", "wl", "g", "w_row", "q1", "heads", "a1_neg", "sums", "a1_exp",
                                               "a1_sum", "a1_rec", "alpha_p1", "p1_columns", "c", "c_scaled", "rowT", "row")}
        w_moved = sem("w_moved")
        row_moved = sem("row_moved")
        w_spread = sem("w_spread")
        row_spread = sem("row_spread")
        xh_done, xs_done = sem("xh_done"), sem("xs_done")
        t_done, s_done, v_done, at_done, av_done = (sem(n) for n in ("t_done", "s_done", "v_done", "at_done", "av_done"))
        th_done, e_done, a_done, vh_done, ah_done = (
            sem(n) for n in ("th_done", "e_done", "a_done", "vh_done", "ah_done"))
        tl_done, shift_done, max_done, top_done, bias_done, rden_done, vl_done, al_done, o_done = (
            sem(n) for n in ("tl_done", "shift_done", "max_done", "top_done", "bias_done", "rden_done",
                             "vl_done", "al_done", "o_done"))
        o_stored = [sem("o_stored0"), sem("o_stored1")]

        g1_ps = vo_ps[:, 0, 1, :].rearrange("p (t n) -> p t n", t=DT)
        g2_ps = vo_ps[:, 1, 0, :].rearrange("p (t n) -> p t n", t=DT)
        z_ps = vo_ps[:, 1, 1, :].rearrange("p (t n) -> p t n", t=DT)
        m_ps = t_ps[:, :, 0:S]

        def pieces(bank):
            flat = bank[:].rearrange("p t n -> p (t n)")
            return [flat[:, n:n + DT * B].rearrange("p (t b) -> p t b", t=DT) for n in range(0, flat.shape[1], DT * B)]

        u_ps, rT_ps, a_ps, kappa_ps, g_ps = pieces(s_ps)[:5]
        a_kappa_ps = pieces(s_ps)[5][:, 0, :]
        q1_ps, k1_ps = pieces(at_ps)[:2]
        a1_ps = pieces(at_ps)[2][:, 0, :]
        c_ps = vo_ps[:, 1, 0, 0:DT * B].rearrange("p (t b) -> p t b", t=DT)
        w_ps = at_ps[0:B, 0, :]
        row_ps = vo_ps[0:B, 1, 1, 0:D]

        def one(i):
            return slice(i, i + 1) if isinstance(i, int) else bass.ds(i, 1)

        def bias_of(name, t):
            return biasT[:, t, BROW[name]:BROW[name] + 1]

        block = ctx.enter_context(nc.Block())

        WARM_UP = 14
        RUNS = [(0, 4), (4, 18), (18, B)]

        @block.sync
        def _(sp):
            def weight(dst, src, name):
                sp.dma_start(dst, src.rearrange("(t p) n -> p t n", p=P)).then_inc(ld[name], 16)

            def load_x(j, slot):
                sp.dma_start(x_nat[:, slot].rearrange("p t d -> p (t d)"), x_rows[j]).then_inc(x_loaded[slot], 16)

            def load_xc(j, slot):
                sp.dma_start(x_col[:, slot], x_columns[j]).then_inc(xc_loaded[slot], 16)

            sp.dma_start(weT_in[:], we_columns).then_inc(ld["weT"], 16)
            weight(wk2_in[:], Wk2, "wk2")
            load_xc(0, 0)
            weight(we_in[:], Wul[D:2 * D, :], "we")
            sp.dma_start(wv_in[:].rearrange("p h t n -> p (h t) n"), Wv.rearrange("(a p) n -> p a n", p=P)).then_inc(ld["wv"], 16)
            load_x(0, 0)
            load_xc(1, 1)
            load_x(1, 1)
            weight(wq1_in[:], Wq1, "wq1")
            weight(wk1_in[:], Wk1, "wk1")

            def load(j, slot):
                sp.wait_ge(xs_done, j - 1)
                load_xc(j, slot)
                sp.wait_ge(shift_done, j - 1)
                load_x(j, slot)

            def store(j, slot):
                sp.wait_ge(o_done, j + 1)
                sp.dma_start(out_rows[j], o_sb[:, slot].rearrange("p t d -> p (t d)")).then_inc(o_stored[slot], 16)

            sp.wait_ge(prep_sb["w_row"], 1)
            sp.dma_start(rows_flat[32:33], w_row[:]).then_inc(w_moved, 16)
            load(2, 0)
            sp.wait_ge(prep_sb["row"], 1)
            sp.dma_start(rows_flat[0:1], row[:]).then_inc(row_moved, 16)
            load(3, 1)
            load(4, 0)
            store(0, 0)
            with sp.Fori(2, B - 4, 2) as i:
                for n in range(2):
                    load(i + (n + 3), (n + 1) % 2)
                    store(i + (n - 1), (n + 1) % 2)
            for i in range(B - 4, B):
                if i + 3 < B:
                    load(i + 3, (i + 1) % 2)
                store(i - 1, (i + 1) % 2)
            for s in range(ST):
                sp.wait_ge(o_done, B + s)
                sp.dma_start(out_rows[B - 1][:, s * D:(s + 1) * D], o_sb[:, 1, s, :]).then_inc(o_stored[1], 16)
            sp.wait_ge(o_stored[0], 16 * (B // 2))
            sp.wait_ge(o_stored[1], 16 * (B // 2 + ST - 1))

        @block.gpsimd
        def _(pool):
            nc.gpsimd.memset(ident[:], 0.0).then_inc(eye_zero, 1)
            pool.wait_ge(eye_zero, 1)
            nc.gpsimd.affine_select(out=ident[:], in_=ident[:], compare_op=ALU.not_equal, fill=1.0,
                                    base=0, pattern=[[-1, P]], channel_multiplier=1).then_inc(eye_made, 1)
            nc.gpsimd.memset(eye[:], 0.0).then_inc(eye_zero, 1)
            pool.wait_ge(eye_zero, 2)
            nc.gpsimd.affine_select(out=eye[:], in_=eye[:], compare_op=ALU.not_equal, fill=1.0,
                                    base=0, pattern=[[P, DT], [-1, D]], channel_multiplier=1).then_inc(eye_made, 1)
            nc.gpsimd.memset(ones[:], 1.0).then_inc(ones_made, 1)

            def split(j, slot, wait=True):
                pool.wait_ge(xc_loaded[slot], (j - slot) * 8 + 16)
                if wait:
                    pool.wait_ge(v_done, j - 1)
                nc.gpsimd.tensor_tensor(x_h[:, slot], x_col[:, slot], zeros[:], ALU.add).then_inc(xh_done, 1)
                pool.wait_ge(xh_done, j + 1)
                nc.gpsimd.tensor_tensor(x_l[:, slot], x_col[:, slot], x_h[:, slot].bitcast(F32), ALU.subtract).then_inc(xs_done, 1)

            def spread(partition, dst, run, done, splits):
                b0, b1 = RUNS[run]
                pool.wait_ge(xs_done, splits)
                nc.gpsimd.partition_broadcast(dst[:, b0:b1, :], rows_flat[partition:partition + 1, b0:b1, :]).then_inc(done, 1)
                pool.wait_ge(done, run + 1)

            nc.gpsimd.memset(zeros[:], 0.0).then_inc(zeros_made, 1)
            pool.wait_ge(zeros_made, 1)
            split(0, 0, False)
            split(1, 1, False)
            pool.wait_ge(w_moved, 16)
            for run in range(len(RUNS)):
                spread(32, w_all, run, w_spread, 2)
            split(2, 0)
            pool.wait_ge(row_moved, 16)
            for run in range(len(RUNS)):
                spread(0, row_all, run, row_spread, 3 + run)
                split(3 + run, (3 + run) % 2)
            with pool.Fori(6, B, 2) as j:
                split(j, 0)
                split(j + 1, 1)

        @block.tensor
        def _(pe):
            mm = nc.tensor.matmul

            def weight_product(dst, lhs, rhs):
                for t in range(DT):
                    for c in range(DT):
                        last = mm(dst[:, t, :], lhs[:, c, t * P:(t + 1) * P], rhs[:, c, :], start=(c == 0), stop=(c == DT - 1))
                return last

            def vector_product(dst, terms):
                for t in range(DT):
                    steps = [(w[:, c, t * P:(t + 1) * P], vT[:, c, :]) for w, vT in terms for c in range(DT)]
                    for n, (w, vT) in enumerate(steps):
                        last = mm(dst[:, t, :], w, vT, start=(n == 0), stop=(n == len(steps) - 1))
                return last

            def feature_sum(dst, products):
                for c in range(DT):
                    last = mm(dst, ones[:], products[:, c, :], start=(c == 0), stop=(c == DT - 1))
                return last

            pe.wait_ge(eye_made, 1)
            for n in range(WARM_UP):
                nc.tensor.transpose(vo_ps[:, 1, 1, 0:P], ident[:], ident[:])

            pe.wait_ge(prep_sb["wT"], 1)
            pe.wait_ge(ld["wq2"], 16)
            weight_product(g1_ps, wq2_in, wT).then_inc(prep_pe["g1"], 1)
            pe.wait_ge(ld["cond"], 16)
            pe.wait_ge(ld["wp"], 16)
            vector_product(u_ps, [(wp_in, condT)]).then_inc(prep_pe["u"], 1)
            pe.wait_ge(ld["wk2"], 16)
            weight_product(g2_ps, wk2_in, wT).then_inc(prep_pe["g2"], 1)
            pe.wait_ge(prep_sb["u"], 1)
            pe.wait_ge(ld["wu"], 16)
            vector_product(rT_ps, [(wu_in, uT)]).then_inc(prep_pe["rT"], 1)
            pe.wait_ge(prep_sb["g1"], 1)
            pe.wait_ge(prep_sb["g2"], 1)
            weight_product(m_ps, g1T, g2T).then_inc(prep_pe["m"], 1)
            pe.wait_ge(prep_sb["rT"], 1)
            vector_product(a_ps, [(wq2_in, rT)])
            vector_product(kappa_ps, [(wk2_in, rT)]).then_inc(prep_pe["a_kappa"], 1)
            def split_product(dst, l_h, l_l, r_h, r_l, first=True):
                steps = [(l, r, c) for c in range(2) for l, r in ((l_h, r_h), (l_h, r_l), (l_l, r_h))]
                for n, (l, r, c) in enumerate(steps):
                    last = mm(dst, l(c), r(c), start=(first and n == 0), stop=(n == len(steps) - 1), skip_group_check=True)
                return last

            def queries(slot):
                for e in range(DT):
                    c0 = slice(e * P, (e + 1) * P)
                    split_product(t_ps[:, e, 0:S], lambda c: m_h[:, c, c0], lambda c: m_l[:, c, c0],
                                  lambda c: x_h[:, slot, c, :], lambda c: x_l[:, slot, c, :]).then_inc(t_done, 1)

            def scores(slot):
                for s in range(ST):
                    c0 = slice(s * P, (s + 1) * P)
                    last = split_product(s_ps[:, s, :], lambda c: t_h[:, c, c0], lambda c: t_l[:, c, c0],
                                         lambda c: x_h[:, slot, c, :], lambda c: x_l[:, slot, c, :])
                last.then_inc(s_done, 1)

            def values(slot, s):
                c0 = slice(s * P, (s + 1) * P)
                return split_product(vo_ps[:, slot, s, :], lambda c: x_h[:, slot, c, c0], lambda c: x_l[:, slot, c, c0],
                                     lambda c: zw_h[:, c, :], lambda c: zw_l[:, c, :])

            def mix(slot, s, high=v_h, low=v_l):
                c0 = slice(s * P, (s + 1) * P)
                return split_product(vo_ps[:, slot, s, D:2 * D], lambda c: a_h[:, c, c0], lambda c: a_l[:, c, c0],
                                     lambda c: high[:, c, :], lambda c: low[:, c, :], first=False)

            def a_transpose():
                for k in range(ST):
                    for s in range(ST):
                        last = nc.tensor.transpose(at_ps[:, k, s * P:(s + 1) * P], a_nat[:, s, k * P:(k + 1) * P], ident[:])
                last.then_inc(at_done, 1)

            def step(i, slot, but=()):
                other = 1 - slot
                pe.wait_ge(tl_done, i + 1)
                scores(slot)
                if "o" not in but:
                    pe.wait_ge(o_done, i - 1)
                if "row" in but:
                    pe.wait_ge(prep_sb["row"], 1)
                values(slot, 0)
                values(slot, 1).then_inc(v_done, 1)
                pe.wait_ge(xs_done, i + 2)
                queries(other)
                pe.wait_ge(vl_done, i)
                pe.wait_ge(al_done, i)
                mix(other, 0)
                mix(other, 1).then_inc(av_done, 1)
                pe.wait_ge(a_done, i + 1)
                a_transpose()

            pe.wait_ge(prep_sb["mh"], 1)
            pe.wait_ge(prep_sb["ml"], 1)
            pe.wait_ge(xs_done, 1)
            queries(0)
            pe.wait_ge(prep_sb["a_kappa"], 1)
            for c in range(DT):
                last = mm(w_ps, kappaT[:, c, :], g1T[:, c, :], start=(c == 0), stop=(c == DT - 1))
            last.then_inc(prep_pe["w_row"], 1)
            vector_product(g_ps, [(g2T, aT)])
            pe.wait_ge(ones_made, 1)
            pe.wait_ge(prep_sb["products"], 1)
            feature_sum(a_kappa_ps, a_kappa).then_inc(prep_pe["g"], 1)
            pe.wait_ge(prep_sb["w_row"], 1)
            pe.wait_ge(ld["wq1"], 16)
            vector_product(q1_ps, [(wq1_in, condT)])
            pe.wait_ge(ld["wk1"], 16)
            vector_product(k1_ps, [(wk1_in, condT)]).then_inc(prep_pe["heads"], 1)
            pe.wait_ge(ld["wv"], 16)
            weight_product(z_ps, wT, wv_in[:, 1]).then_inc(prep_pe["z"], 1)
            pe.wait_ge(prep_sb["heads"], 1)
            feature_sum(a1_ps, q1_k1).then_inc(prep_pe["sums"], 1)

            pe.wait_ge(prep_sb["g"], 1)
            pe.wait_ge(tl_done, 1)
            scores(0)
            vector_product(c_ps, [(wv_in[:, 0], condT), (wv_in[:, 1], rT)]).then_inc(prep_pe["c"], 1)
            pe.wait_ge(xs_done, 2)
            queries(1)
            for n in ("zh", "zl", "wh", "wl"):
                pe.wait_ge(prep_sb[n], 1)
            values(0, 0)
            values(0, 1).then_inc(v_done, 1)
            pe.wait_ge(prep_sb["rowT"], 1)
            for c in range(DT):
                last = nc.tensor.transpose(row_ps[:, c * P:(c + 1) * P], rowT[:, c, :], ident[:])
            last.then_inc(prep_pe["row"], 1)
            pe.wait_ge(a_done, 1)
            a_transpose()

            step(1, 1, ("o", "row"))
            with pe.Fori(2, B - 2, 2) as i:
                step(i, 0)
                step(i + 1, 1)
            step(B - 2, 0)
            pe.wait_ge(tl_done, B)
            scores(1)
            pe.wait_ge(o_done, B - 2)
            for s in range(ST):
                values(1, s).then_inc(v_done, 1)
            pe.wait_ge(vl_done, B - 1)
            pe.wait_ge(al_done, B - 1)
            for s in range(ST):
                last = mix(0, s)
                if s == ST - 1:
                    last.then_inc(av_done, 1)
                pe.wait_ge(a_done, B + s)
                for k in range(ST):
                    last = nc.tensor.transpose(tail_ps[s][:, k, :], a_nat[:, s, k * P:(k + 1) * P], ident[:])
                last.then_inc(at_done, 1)
            pe.wait_ge(vl_done, B + ST - 1)
            for s in range(ST):
                pe.wait_ge(al_done, B + s)
                mix(1, s, v_last_h, v_last_l).then_inc(av_done, 1)

        @block.scalar
        def _(act):
            copy, activation = nc.scalar.copy, nc.scalar.activation

            act.dma_start(wq2_in[:], Wq2.rearrange("(t p) n -> p t n", p=P)).then_inc(ld["wq2"], 16)
            act.dma_start(condT[:], cond_columns).then_inc(ld["cond"], 16)
            act.dma_start(wp_in[:], Wp.rearrange("(t p) n -> p t n", p=P)).then_inc(ld["wp"], 16)
            act.dma_start(biasT[:], bias_columns).then_inc(ld["bias"], 16)
            act.dma_start(wu_in[:], Wul[0:D, :].rearrange("(t p) n -> p t n", p=P)).then_inc(ld["wu"], 16)
            act.dma_start(alpha_in[:], alpha.rearrange("(a n) -> a n", a=1).to_broadcast([P, 1])).then_inc(ld["alpha"], 16)
            act.wait_ge(eye_made, 1)
            activation(warm[:, 0:1], ident[:, 0:1], ACT.Gelu)
            act.wait_ge(prep_pe["u"], 1)
            act.wait_ge(ld["bias"], 16)
            for t in range(DT):
                last = activation(uT[:, t, :], u_ps[:, t, :], ACT.Gelu, bias=bias_of("bp", t))
            last.then_inc(prep_sb["u"], 1)
            act.wait_ge(prep_pe["g2"], 1)
            copy(g2T[:], g2_ps).then_inc(prep_sb["g2"], 1)
            activation(warm[:, 1:2], ident[:, 0:1], ACT.Exp)
            act.wait_ge(prep_sb["wnat"], 1)
            copy(zw_h[:, :, D:2 * D], w_nat[:]).then_inc(prep_sb["wh"], 1)

            def t_high(i):
                for e in range(DT):
                    act.wait_ge(t_done, DT * i + e + 1)
                    activation(t_h[:, e, :], t_ps[:, e, 0:S], ACT.Identity, bias=gT[:, i, e:e + 1]).then_inc(th_done, 1)

            def exponent(i):
                act.wait_ge(bias_done, i + 1)
                for s in range(ST):
                    last = activation(e_nat[:, s, :], s_ps[:, s, :], ACT.Exp, bias=exp_bias[:, s:s + 1],
                                      accum_out=den[:, s:s + 1])
                last.then_inc(e_done, 1)

            def normalise(i):
                act.wait_ge(rden_done, i + 1)
                for s in range(ST):
                    last = activation(a_nat[:, s, :], e_nat[:, s, :], ACT.Identity, bias=neg_alpha_p1[:, one(i)],
                                      scale=r_den[:, s:s + 1])
                last.then_inc(a_done, 1)

            act.wait_ge(prep_pe["m"], 1)
            copy(m_h[:], m_ps).then_inc(prep_sb["mh"], 1)
            act.wait_ge(prep_pe["w_row"], 1)
            copy(w_row[:], w_ps).then_inc(prep_sb["w_row"], 1)
            act.wait_ge(prep_sb["g"], 1)
            t_high(0)
            act.wait_ge(prep_pe["z"], 1)
            copy(zw_h[:, :, 0:D], z_ps).then_inc(prep_sb["zh"], 1)
            act.wait_ge(prep_sb["sums"], 1)
            activation(a1_exp[:], a1_diff[:], ACT.Exp).then_inc(prep_sb["a1_exp"], 1)
            exponent(0)
            act.wait_ge(prep_sb["p1_columns"], 1)
            normalise(0)
            t_high(1)

            def step(i, slot):
                act.wait_ge(at_done, i)
                copy(a_h[:], at_ps[:]).then_inc(ah_done, 1)
                act.wait_ge(v_done, i)
                copy(v_h[:], vo_ps[:, 1 - slot, :, 0:D]).then_inc(vh_done, 1)
                exponent(i)
                normalise(i)
                t_high(i + 1)

            step(1, 1)
            with act.Fori(2, B - 2, 2) as i:
                step(i, 0)
                step(i + 1, 1)
            step(B - 2, 0)
            act.wait_ge(at_done, B - 1)
            copy(a_h[:], at_ps[:]).then_inc(ah_done, 1)
            act.wait_ge(v_done, B - 1)
            copy(v_h[:], vo_ps[:, 0, :, 0:D]).then_inc(vh_done, 1)
            act.wait_ge(bias_done, B)
            for s in range(ST):
                activation(e_nat[:, s, :], s_ps[:, s, :], ACT.Exp, bias=exp_bias[:, s:s + 1],
                           accum_out=den[:, s:s + 1]).then_inc(e_done, 1)
            for s in range(ST):
                act.wait_ge(rden_done, B + s)
                activation(a_nat[:, s, :], e_nat[:, s, :], ACT.Identity, bias=neg_alpha_p1[:, B - 1:B],
                           scale=r_den[:, s:s + 1]).then_inc(a_done, 1)
                act.wait_ge(v_done, B + s)
                copy(v_last_h[:, s, :], vo_ps[:, 1, s, 0:D]).then_inc(vh_done, 1)
            for s in range(ST):
                act.wait_ge(at_done, B + s)
                copy(a_h[:, :, s * P:(s + 1) * P], tail_ps[s]).then_inc(ah_done, 1)

        @block.vector
        def _(dve):
            tt, ts, stt = nc.vector.tensor_tensor, nc.vector.tensor_scalar, nc.vector.scalar_tensor_tensor

            def low(dst, src, high):
                return tt(dst, src, high.bitcast(F32), ALU.subtract)

            def t_low(i):
                for e in range(DT):
                    dve.wait_ge(th_done, DT * i + e + 1)
                    last = stt(out=t_l[:, e, :], in0=t_ps[:, e, 0:S], scalar=gT[:, i, e:e + 1],
                               in1=t_h[:, e, :].bitcast(F32), op0=ALU.add, op1=ALU.subtract)
                last.then_inc(tl_done, 1)

            def a_low(i):
                dve.wait_ge(ah_done, i + 1)
                low(a_l[:], at_ps[:], a_h[:]).then_inc(al_done, 1)

            def v_low(i, slot):
                dve.wait_ge(vh_done, i + 1)
                low(v_l[:], vo_ps[:, slot, :, 0:D], v_h[:]).then_inc(vl_done, 1)

            def shifts(i, slot):
                dve.wait_ge(x_loaded[slot], (i - slot) * 8 + 16)
                for s in range(ST):
                    last = stt(out=x_w[:, s, :], in0=x_nat[:, slot, s, :], scalar=1.0, in1=w_all[:, one(i), :].rearrange("p o n -> p (o n)"),
                               op0=ALU.mult, op1=ALU.mult, accum_out=shift[:, slot, s:s + 1])
                last.then_inc(shift_done, 1)

            def maximum(i):
                dve.wait_ge(s_done, i + 1)
                nc.vector.tensor_reduce(neg_max[:], s_ps[:], AX.X, ALU.max, negate=True).then_inc(max_done, 1)

            def exponent_bias(i, slot):
                dve.wait_ge(shift_done, i + 1)
                dve.wait_ge(max_done, i + 1)
                stt(out=neg_top[:], in0=neg_max[:], scalar=a_kappa_col[:, one(i)], in1=shift[:, slot, :],
                    op0=ALU.subtract, op1=ALU.subtract).then_inc(top_done, 1)
                dve.wait_ge(top_done, i + 1)
                stt(out=exp_bias[:], in0=neg_top[:], scalar=a_kappa_col[:, one(i)], in1=shift[:, slot, :],
                    op0=ALU.add, op1=ALU.add).then_inc(bias_done, 1)

            def denominator(i):
                dve.wait_ge(e_done, i + 1)
                nc.vector.reciprocal(r_den[:], den[:]).then_inc(rden_done, 1)

            def output(j, slot, wait=True):
                dve.wait_ge(av_done, j + 1)
                if wait:
                    dve.wait_ge(o_stored[slot], (j - slot) * 8)
                tt(o_sb[:, slot], vo_ps[:, slot, :, D:2 * D], row_all[:, one(j), :].to_broadcast([P, ST, D]),
                   ALU.add).then_inc(o_done, 1)

            dve.wait_ge(eye_made, 2)
            dve.wait_ge(ld["weT"], 16)
            tt(wT[:], weT_in[:], eye[:], ALU.add).then_inc(prep_sb["wT"], 1)
            dve.wait_ge(ld["we"], 16)
            tt(w_nat[:], we_in[:], eye[:], ALU.add).then_inc(prep_sb["wnat"], 1)
            dve.wait_ge(prep_pe["g1"], 1)
            ts(g1T[:], g1_ps, SCALE, None, ALU.mult).then_inc(prep_sb["g1"], 1)
            dve.wait_ge(prep_pe["rT"], 1)
            nc.vector.tensor_copy(rT[:], rT_ps).then_inc(prep_sb["rT"], 1)
            dve.wait_ge(prep_sb["wh"], 1)
            low(zw_l[:, :, D:2 * D], w_nat[:], zw_h[:, :, D:2 * D]).then_inc(prep_sb["wl"], 1)
            dve.wait_ge(prep_sb["mh"], 1)
            low(m_l[:], m_ps, m_h[:]).then_inc(prep_sb["ml"], 1)
            dve.wait_ge(prep_pe["a_kappa"], 1)
            dve.wait_ge(ld["bias"], 16)
            for t in range(DT):
                ts(aT[:, t, :], a_ps[:, t, :], bias_of("bq2", t), SCALE, ALU.add, ALU.mult)
                last = ts(kappaT[:, t, :], kappa_ps[:, t, :], bias_of("bk2", t), None, ALU.add)
            last.then_inc(prep_sb["a_kappa"], 1)
            dve.wait_ge(prep_sb["a_kappa"], 1)
            tt(a_kappa[:], aT[:], kappaT[:], ALU.mult).then_inc(prep_sb["products"], 1)
            dve.wait_ge(prep_pe["g"], 1)
            nc.vector.tensor_copy(a_kappa_col[:], a_kappa_ps)
            nc.vector.tensor_copy(gT[:].rearrange("p b t -> p t b"), g_ps).then_inc(prep_sb["g"], 1)
            t_low(0)
            dve.wait_ge(prep_pe["heads"], 1)
            for t in range(DT):
                last = ts(q1T[:, t, :], q1_ps[:, t, :], bias_of("bq1", t), None, ALU.add)
            last.then_inc(prep_sb["q1"], 1)
            dve.wait_ge(prep_sb["q1"], 1)
            for t in range(DT):
                last = stt(out=q1_k1[:, t, :], in0=k1_ps[:, t, :], scalar=bias_of("bk1", t), in1=q1T[:, t, :],
                           op0=ALU.add, op1=ALU.mult)
            last.then_inc(prep_sb["heads"], 1)
            dve.wait_ge(prep_sb["zh"], 1)
            low(zw_l[:, :, 0:D], z_ps, zw_h[:, :, 0:D]).then_inc(prep_sb["zl"], 1)
            dve.wait_ge(prep_pe["sums"], 1)
            ts(a1_neg[:], a1_ps, -SCALE, None, ALU.mult).then_inc(prep_sb["a1_neg"], 1)
            dve.wait_ge(prep_sb["a1_neg"], 1)
            stt(out=a1_diff[:], in0=a1_ps, scalar=SCALE, in1=a1_neg[:], op0=ALU.mult, op1=ALU.add)\
                .then_inc(prep_sb["sums"], 1)
            dve.wait_ge(w_spread, 1)
            shifts(0, 0)
            maximum(0)
            dve.wait_ge(prep_sb["g"], 1)
            exponent_bias(0, 0)
            dve.wait_ge(prep_sb["a1_exp"], 1)
            ts(a1_sum[:], a1_exp[:], float(S), None, ALU.mult).then_inc(prep_sb["a1_sum"], 1)
            dve.wait_ge(prep_sb["a1_sum"], 1)
            nc.vector.reciprocal(a1_rec[:], a1_sum[:]).then_inc(prep_sb["a1_rec"], 1)
            dve.wait_ge(prep_sb["a1_rec"], 1)
            dve.wait_ge(ld["alpha"], 16)
            stt(out=alpha_p1[:], in0=a1_exp[:], scalar=alpha_in[:], in1=a1_rec[:], op0=ALU.mult, op1=ALU.mult)\
                .then_inc(prep_sb["alpha_p1"], 1)
            dve.wait_ge(prep_sb["alpha_p1"], 1)
            ts(neg_alpha_p1[:], alpha_p1[:], -1.0, None, ALU.mult)
            ts(a_row_sum[:], alpha_p1[:], -float(S), 1.0, ALU.mult, ALU.add).then_inc(prep_sb["p1_columns"], 1)
            denominator(0)
            dve.wait_ge(prep_pe["c"], 1)
            for t in range(DT):
                last = ts(cT[:, t, :], c_ps[:, t, :], bias_of("bv", t), None, ALU.add)
            last.then_inc(prep_sb["c"], 1)
            dve.wait_ge(prep_sb["c"], 1)
            dve.wait_ge(prep_sb["p1_columns"], 1)
            for t in range(DT):
                last = tt(cT[:, t, :], cT[:, t, :], a_row_sum[:], ALU.mult)
            last.then_inc(prep_sb["c_scaled"], 1)
            dve.wait_ge(prep_sb["c_scaled"], 1)
            tt(rowT[:], cT[:], rT[:], ALU.add).then_inc(prep_sb["rowT"], 1)
            t_low(1)
            shifts(1, 1)
            dve.wait_ge(prep_pe["row"], 1)
            nc.vector.tensor_copy(row[:], row_ps).then_inc(prep_sb["row"], 1)

            def step(i, slot, but=()):
                a_low(i - 1)
                maximum(i)
                exponent_bias(i, slot)
                v_low(i - 1, 1 - slot)
                denominator(i)
                shifts(i + 1, 1 - slot)
                t_low(i + 1)
                if "row" in but:
                    dve.wait_ge(row_spread, 1)
                output(i - 1, 1 - slot, "first" not in but)

            step(1, 1, ("first", "row"))
            step(2, 0, ("first",))
            dve.wait_ge(w_spread, len(RUNS))
            step(3, 1)
            dve.wait_ge(row_spread, len(RUNS))
            with dve.Fori(4, B - 2, 2) as i:
                step(i, 0)
                step(i + 1, 1)
            step(B - 2, 0)
            a_low(B - 2)
            maximum(B - 1)
            exponent_bias(B - 1, 1)
            v_low(B - 2, 0)
            for s in range(ST):
                dve.wait_ge(e_done, B + s)
                nc.vector.reciprocal(r_den[:, s:s + 1], den[:, s:s + 1]).then_inc(rden_done, 1)
            for s in range(ST):
                dve.wait_ge(vh_done, B + s)
                low(v_last_l[:, s, :], vo_ps[:, 1, s, 0:D], v_last_h[:, s, :]).then_inc(vl_done, 1)
            for s in range(ST):
                dve.wait_ge(ah_done, B + s)
                low(a_l[:, :, s * P:(s + 1) * P], tail_ps[s], a_h[:, :, s * P:(s + 1) * P]).then_inc(al_done, 1)
            output(B - 2, 0)
            dve.wait_ge(o_stored[1], (B - 2) * 8)
            for s in range(ST):
                dve.wait_ge(av_done, B + s)
                tt(o_sb[:, 1, s, :], vo_ps[:, 1, s, D:2 * D], row_all[:, B - 1, :], ALU.add).then_inc(o_done, 1)


_INS = ["x", "L0_cond_weight_matrix", "L0_cond_W_proj", "L1_cond_Wq1", "L1_cond_Wq2", "L1_cond_Wk1", "L1_cond_Wk2",
        "L1_cond_Wv", "L1_cond_alpha"]
_BIASES = ["L0_cond_b_proj", "L1_cond_bq1", "L1_cond_bk1", "L1_cond_bq2", "L1_cond_bk2", "L1_cond_bv"]


def _columns(a):
    return a.T.reshape(a.shape[1] // P, P, a.shape[0]).transpose(1, 0, 2)


def kernel(**inputs):
    import numpy as _np
    import concourse.bacc as _bacc
    from concourse import mybir as _mybir
    from concourse.bass_utils import run_bass_kernel_spmd as _run

    nc = _bacc.Bacc("TRN2", target_bir_lowering=False, num_devices=1)
    arrays, args = {}, []
    laid_out = {name: inputs[name] for name in _INS}
    x = _np.asarray(inputs["x"])
    b, s, d = x.shape
    laid_out["x_columns"] = x.reshape(b, P, s // P, d // P, P).transpose(0, 4, 3, 2, 1).reshape(b, P, d // P, s)
    laid_out["we_columns"] = _columns(_np.asarray(inputs["L0_cond_weight_matrix"])[d:])
    laid_out["cond_columns"] = _columns(_np.asarray(inputs["cond_1024"]))
    laid_out["bias_columns"] = _columns(_np.stack([_np.asarray(inputs[name]) for name in _BIASES]))
    for name, a in laid_out.items():
        a = _np.ascontiguousarray(a)
        arrays[f"in_{name}"] = a
        args.append(nc.dram_tensor(f"in_{name}", a.shape, _mybir.dt.from_np(a.dtype), kind="ExternalInput").ap())
    out = nc.dram_tensor("out_0", arrays["in_x"].shape, _mybir.dt.float32, kind="ExternalOutput").ap()
    build(nc, *args, out)
    r = _run(nc, [arrays], core_ids=[0])
    return r.results[0]["out_0"]
```
